# Optimizing a Trainium2 kernel written in Bass

```python
import numpy as np
import jax
import jax.numpy as jnp

def _softmax(x, axis=-1):
    return jax.nn.softmax(x, axis=axis)

def _gelu(x):
    return jax.nn.gelu(x, approximate=True)

def _silu(x):
    return jax.nn.silu(x)

def _sigmoid(x):
    return jax.nn.sigmoid(x)

def _layernorm(x, axis=-1, eps=1e-05):
    m = jnp.mean(x, axis=axis, keepdims=True)
    v = jnp.var(x, axis=axis, keepdims=True)
    return (x - m) / jnp.sqrt(v + eps)

def _scatter_add(tgt, idx, src, axis=0):
    return tgt.at[idx].add(src)

def _segment_sum(src, seg, n):
    return jax.ops.segment_sum(src, seg, n)
kernel_name = 'mk_cond_seq_d1_seqx_r4_10689e'

def setup_inputs(seed: int=0):
    np.random.seed(seed)
    _w = jnp.asarray

    def _rec_inputs():
        import jax
        import jax.numpy as jnp
        _rk = jax.random.key(seed)
        x = -0.0002928 + 1 * jax.random.normal(jax.random.fold_in(_rk, 1), (128, 64, 256), jnp.float32)
        _lenS = 64 - jax.random.randint(jax.random.fold_in(_rk, 7), (128,), 0, max(1, 64 // 4) + 1, jnp.int32)
        _lenS2 = 64 - jax.random.randint(jax.random.fold_in(_rk, 8), (128,), 0, max(1, 64 // 4) + 1, jnp.int32)
        cond_1024 = 0.000887014 + 1.03683 * jax.random.normal(jax.random.fold_in(_rk, 11), (128, 256), jnp.float32)
        return (x, cond_1024)
    x, cond_1024 = _rec_inputs()

    def _L0_cond_setup():
        import jax, jax.numpy as jnp
        import numpy as np
        DIM = 256
        HEADS = 16
        HEAD_DIM = DIM // HEADS
        MLP = 4 * DIM
        EPS = 1e-05

        def layer_norm(x, g, b):
            mu = jnp.mean(x, axis=-1, keepdims=True)
            var = jnp.var(x, axis=-1, keepdims=True)
            return (x - mu) * jax.lax.rsqrt(var + EPS) * g + b

        def rope_cos_sin(n, d):
            inv_freq = 1.0 / 10000.0 ** (jnp.arange(0, d, 2, dtype=jnp.float32) / d)
            t = jnp.arange(n, dtype=jnp.float32)
            freqs = jnp.outer(t, inv_freq)
            emb = jnp.concatenate([freqs, freqs], -1)
            return (jnp.cos(emb), jnp.sin(emb))

        def rotate_half(x):
            x1, x2 = (x[..., ::2], x[..., 1::2])
            return jnp.concatenate([-x2, x1], axis=-1)
        key = jax.random.key(seed)
        ks = jax.random.split(key, 16)
        B, N = (2, 512)
        s = lambda fan_in: 1.0 / np.sqrt(fan_in)
        inp = {'x': jax.random.normal(ks[0], (B, N, DIM), jnp.float32), 't_emb': jax.random.normal(ks[1], (B, DIM), jnp.float32), 'norm1_g': jnp.ones((DIM,), jnp.float32), 'norm1_b': jnp.zeros((DIM,), jnp.float32), 'Wq': jax.random.normal(ks[2], (DIM, DIM), jnp.float32) * s(DIM), 'Wk': jax.random.normal(ks[3], (DIM, DIM), jnp.float32) * s(DIM), 'Wv': jax.random.normal(ks[4], (DIM, DIM), jnp.float32) * s(DIM), 'Wo': jax.random.normal(ks[5], (DIM, DIM), jnp.float32) * s(DIM), 'norm2_g': jnp.ones((DIM,), jnp.float32), 'norm2_b': jnp.zeros((DIM,), jnp.float32), 'W1': jax.random.normal(ks[6], (DIM, MLP), jnp.float32) * s(DIM), 'W2': jax.random.normal(ks[7], (MLP, DIM), jnp.float32) * s(MLP), 'ada_W': jax.random.normal(ks[8], (DIM, 6 * DIM), jnp.float32) * s(DIM), 'ada_b': jnp.zeros((6 * DIM,), jnp.float32)}
        return inp
    _L0_cond_all = _L0_cond_setup()
    _L0_cond_in = {k: v for k, v in _L0_cond_all.items() if k in ('norm1_g', 'norm1_b', 'Wq', 'Wk', 'Wv', 'Wo', 'norm2_g', 'norm2_b', 'W1', 'W2', 'ada_W', 'ada_b')}
    del _L0_cond_all
    return {'x': x, 'cond_1024': cond_1024, 'L0_cond_norm1_g': _L0_cond_in['norm1_g'], 'L0_cond_norm1_b': _L0_cond_in['norm1_b'], 'L0_cond_Wq': _L0_cond_in['Wq'], 'L0_cond_Wk': _L0_cond_in['Wk'], 'L0_cond_Wv': _L0_cond_in['Wv'], 'L0_cond_Wo': _L0_cond_in['Wo'], 'L0_cond_norm2_g': _L0_cond_in['norm2_g'], 'L0_cond_norm2_b': _L0_cond_in['norm2_b'], 'L0_cond_W1': _L0_cond_in['W1'], 'L0_cond_W2': _L0_cond_in['W2'], 'L0_cond_ada_W': _L0_cond_in['ada_W'], 'L0_cond_ada_b': _L0_cond_in['ada_b']}

def reference(x, cond_1024, L0_cond_norm1_g, L0_cond_norm1_b, L0_cond_Wq, L0_cond_Wk, L0_cond_Wv, L0_cond_Wo, L0_cond_norm2_g, L0_cond_norm2_b, L0_cond_W1, L0_cond_W2, L0_cond_ada_W, L0_cond_ada_b):
    import jax
    import jax.numpy as jnp

    def _L0_cond_ref(x, t_emb, norm1_g, norm1_b, Wq, Wk, Wv, Wo, norm2_g, norm2_b, W1, W2, ada_W, ada_b):
        import jax, jax.numpy as jnp
        import numpy as np
        DIM = 256
        HEADS = 16
        HEAD_DIM = DIM // HEADS
        MLP = 4 * DIM
        EPS = 1e-05

        def layer_norm(x, g, b):
            mu = jnp.mean(x, axis=-1, keepdims=True)
            var = jnp.var(x, axis=-1, keepdims=True)
            return (x - mu) * jax.lax.rsqrt(var + EPS) * g + b

        def rope_cos_sin(n, d):
            inv_freq = 1.0 / 10000.0 ** (jnp.arange(0, d, 2, dtype=jnp.float32) / d)
            t = jnp.arange(n, dtype=jnp.float32)
            freqs = jnp.outer(t, inv_freq)
            emb = jnp.concatenate([freqs, freqs], -1)
            return (jnp.cos(emb), jnp.sin(emb))

        def rotate_half(x):
            x1, x2 = (x[..., ::2], x[..., 1::2])
            return jnp.concatenate([-x2, x1], axis=-1)
        B, N, C = x.shape
        H, D = (HEADS, HEAD_DIM)
        scale = D ** (-0.5)
        mod = jax.nn.silu(t_emb) @ ada_W + ada_b
        shift_msa, scale_msa, gate_msa, shift_mlp, scale_mlp, gate_mlp = jnp.split(mod, 6, axis=-1)
        xn = layer_norm(x, norm1_g, norm1_b) * (1 + scale_msa[:, None, :]) + shift_msa[:, None, :]
        q = (xn @ Wq).reshape(B, N, H, D).transpose(0, 2, 1, 3)
        k = (xn @ Wk).reshape(B, N, H, D).transpose(0, 2, 1, 3)
        v = (xn @ Wv).reshape(B, N, H, D).transpose(0, 2, 1, 3)
        cos, sin = rope_cos_sin(N, D)
        q = q * cos + rotate_half(q) * sin
        k = k * cos + rotate_half(k) * sin
        attn = jnp.einsum('bhnd,bhmd->bhnm', q, k) * scale
        attn = jax.nn.softmax(attn, axis=-1)
        out = jnp.einsum('bhnm,bhmd->bhnd', attn, v)
        out = out.transpose(0, 2, 1, 3).reshape(B, N, C) @ Wo
        x = x + gate_msa[:, None, :] * out
        xn = layer_norm(x, norm2_g, norm2_b) * (1 + scale_mlp[:, None, :]) + shift_mlp[:, None, :]
        mlp = jax.nn.gelu(xn @ W1, approximate=False) @ W2
        x = x + gate_mlp[:, None, :] * mlp
        return x
    x = _L0_cond_ref(x, cond_1024, L0_cond_norm1_g, L0_cond_norm1_b, L0_cond_Wq, L0_cond_Wk, L0_cond_Wv, L0_cond_Wo, L0_cond_norm2_g, L0_cond_norm2_b, L0_cond_W1, L0_cond_W2, L0_cond_ada_W, L0_cond_ada_b)
    return x

_drawn_inputs = setup_inputs


def setup_inputs(seed=0):
    import zlib

    import numpy as np

    out = dict(_drawn_inputs(seed))
    spreads = {'L0_cond_norm1_g': (1.0, 0.2),
     'L0_cond_norm1_b': (0.0, 0.1),
     'L0_cond_norm2_g': (1.0, 0.2),
     'L0_cond_norm2_b': (0.0, 0.1),
     'L0_cond_ada_b': (0.0, 0.1)}
    factors = {}
    for name, (base, spread) in spreads.items():
        noise = np.random.default_rng([zlib.crc32(name.encode()), seed]).standard_normal(out[name].shape)
        drawn = base * np.exp(spread * noise) if base else spread * noise
        out[name] = jnp.asarray(drawn.astype(out[name].dtype))
    for name, factor in factors.items():
        out[name] = (out[name] * factor).astype(out[name].dtype)
    return out
```

```python
from contextlib import ExitStack

import numpy as np

import concourse.bass as bass
from concourse import mybir

F32 = mybir.dt.float32
F16 = mybir.dt.float16
ALU = mybir.AluOpType
ACT = mybir.ActivationFunctionType
AX_X = mybir.AxisListType.X

P = 128
B, N, C = 128, 64, 256
H, D = 16, 16
F = 4 * C
KT = C // P
GB = 8
G = B // GB
T = 4
I = P // GB
GT = GB * N
J = H // 2
JK = J // KT
BP = GB // 2
FU = F // P
D1 = D + 1
EPS = 1e-5

W_SCALE = 64.0
V_SCALE = 4.0
X_SCALE = 16.0
QK_SCALE = 4.0
ROPE_SCALE = QK_SCALE / (W_SCALE * X_SCALE)
EXP_SCALE = D ** -0.5 / (QK_SCALE * QK_SCALE)
MAX_SCALE = QK_SCALE * QK_SCALE
O_SCALE = V_SCALE * X_SCALE
GATE1_SCALE = 1.0 / (O_SCALE * W_SCALE)
GATE2_SCALE = 1.0 / W_SCALE
GELU_SCALE = 1.0 / (W_SCALE * X_SCALE)


def build(nc, x, cond, g1, b1, wq, wk, wv, wo, g2, b2, w1, w2, ada_w, ada_b, rope, out):
    ctx = ExitStack()
    with ctx:
        def sb(name, shape, dt):
            return ctx.enter_context(nc.sbuf_tensor(name, shape, dt))

        def psum(name, shape, dt):
            return ctx.enter_context(nc.psum_tensor(name, shape, dt))

        def sem(name):
            return ctx.enter_context(nc.semaphore(name))

        x_g = x.rearrange("(g b) (i t) c -> g (b i) (t c)", b=GB, t=T)
        out_g = out.rearrange("(g b) (i t) c -> g (b i) (t c)", b=GB, t=T)
        mod_dram = nc.dram_tensor("mod_scratch", (B, 6, C), F32).ap()
        mod_g = mod_dram.rearrange("(g b) s c -> g b s c", b=GB)

        w_qk = sb("w_qk", [P, 2, 4, KT, C], F16)
        w_v = sb("w_v", [P, 2, KT, C], F16)
        w_o = sb("w_o", [P, 2, KT, C], F16)
        w_1 = sb("w_1", [P, 2, KT, F], F16)
        w_2 = sb("w_2", [P, 2, FU, C], F16)
        ident16 = sb("ident16", [P, P], F16)
        ident32 = sb("ident32", [P, P], F32)
        table = sb("table", [P, 2 * N + 2], F32)
        rope_sb = table[:, 0:2 * N].rearrange("p (s n) -> p s n", s=2)
        parity = table[:, 2 * N:2 * N + 2]
        minus_half = sb("minus_half", [P, T], F32)

        x_in = sb("x_in", [P, T, C], F32)
        x_res = sb("x_res", [P, T, C], F32)
        x_mid = sb("x_mid", [P, T, C], F32)
        out_sb = sb("out_sb", [P, T, C], F32)
        mod1 = sb("mod1", [P, 2, C], F32)
        mod2 = sb("mod2", [P, 3, C], F32)
        mod3 = sb("mod3", [P, 1, C], F32)
        stats = sb("stats", [P, 2, T, 6], F32)
        moments = sb("moments", [P, 2, T, 2], F32)
        var_eps = sb("var_eps", [P, 2, T], F32)
        rstd = sb("rstd", [P, 2, T], F32)
        n1_32 = sb("n1_32", [P, T, C], F32)
        n1_16 = sb("n1_16", [P, T, 2, C], F16)
        n2_32 = sb("n2_32", [P, T, C], F32)
        n2_16 = sb("n2_16", [P, T, 2, C], F16)
        n1T = sb("n1T", [P, 2, KT, GT], F16)
        n2T = sb("n2T", [P, 2, KT, GT], F16)
        rope_c = sb("rope_c", [P, 2, GT], F32)
        rope_s = sb("rope_s", [P, 2, GT], F32)
        qk_32 = sb("qk_32", [P, 2, GT], F32)
        q_16 = sb("q_16", [P, KT, 2, GT], F16)
        k_16 = sb("k_16", [P, KT, 2, GB, 2, N], F16)
        q_stack = sb("q_stack", [P, J, GT], F16)
        k_stack = sb("k_stack", [P, J, GB, 2, N], F16)
        v_16 = sb("v_16", [P, BP, 2, 2, J, D1], F16)
        v_diag = sb("v_diag", [P, GB, 2, 2, J, D1], F16)
        smax = sb("smax", [P, BP, H], F32)
        smaxT = sb("smaxT", [H, GT], F16)
        p_32 = sb("p_32", [P, 2, J * N], F32)
        p_16 = sb("p_16", [P, 4, 2, J * N], F16)
        rsum = sb("rsum", [P, BP, H], F32)
        o_32 = sb("o_32", [P, 2, C], F32)
        o_16 = sb("o_16", [P, BP, 2, C], F16)
        oT = sb("oT", [P, 2, KT, GT], F16)
        gated = sb("gated", [P, 2, C], F32)
        h_32 = sb("h_32", [P, 3, GT], F32)
        h_16 = sb("h_16", [P, FU, 2, GT], F16)

        ps_proj = [psum(f"ps_proj{n}", [P, GT], F32) for n in range(2)]
        ps_tok = [psum(f"ps_tok{n}", [P, 512], F32)[:, 0:C] for n in range(2)]
        ps_score = [psum(f"ps_score{n}", [P, 512], F32) for n in range(2)]
        ps_turn = [ps[:, 0:C].bitcast(F16).rearrange("p (h k n) -> p h k n", h=2, k=KT) for ps in ps_score]
        ps_pv = [psum(f"ps_pv{n}", [P, 512], F32) for n in range(2)]
        pv_out = [ps[:, 0:J * 2 * D1].rearrange("p (h e) -> p h e", e=D1) for ps in ps_pv]
        ps_smaxT = [ps[0:H, 384:384 + P] for ps in ps_pv]

        stage_h = h_16[:].rearrange("p u a n -> p (u a n)").bitcast(F32)
        stage_w1 = stage_h[:, 0:KT * F].rearrange("p (k n) -> p k n", k=KT)
        stage_w2 = stage_h[:, KT * F:KT * F + FU * C].rearrange("p (u n) -> p u n", u=FU)
        stage_q = q_stack[:].rearrange("p j n -> p (j n)").bitcast(F32)
        stage_qkvo = stage_q.rearrange("p (w k n) -> p w k n", w=4, k=KT)
        stage_k = k_stack[:].rearrange("p j b a n -> p (j b a n)").bitcast(F32)
        stage_ada = stage_k[:, 0:KT * 6 * C].rearrange("p (k n) -> p k n", k=KT)
        stage_norm = stage_k[:, KT * 6 * C:KT * 6 * C + 4 * C].rearrange("p (s n) -> p s n", s=4)
        stage_mod = oT[:].rearrange("p h k n -> p (h k n)").bitcast(F32)
        stage_mod2 = n1T[:].rearrange("p h k n -> p (h k n)").bitcast(F32)
        stage_mod = stage_mod.rearrange("p (s n) -> p s n", n=C)
        stage_mod2 = stage_mod2.rearrange("p (s n) -> p s n", n=C)[:, 0:2]

        def mod_row(s):
            return stage_mod[:, s] if s < 4 else stage_mod2[:, s - 4]

        mod_out = p_16[:].rearrange("p a h n -> p (a h n)").bitcast(F32)[:, 0:6 * C]
        mod_out = mod_out.rearrange("p (s n) -> p s n", s=6)
        cond_sb = n1_32[:, 0, :]
        cond_e = n1_32[:, 1, :]
        cond_r = n1_32[:, 2, :]
        cond_s = n1_32[:, 3, :]
        condT = n2_32[:, 0, :].rearrange("p (k b) -> p k b", k=KT)
        ada_b_sb = h_32[:].rearrange("p a n -> p (a n)")[:, 0:6 * C].rearrange("p (s n) -> p s n", s=6)

        cond_in = sem("cond_in")
        ada_in = sem("ada_in")
        wqkvo_in = sem("wqkvo_in")
        wmlp_in = sem("wmlp_in")
        rope_in = sem("rope_in")
        zeroed = sem("zeroed")
        ident_done = sem("ident_done")
        cond_exp = sem("cond_exp")
        cond_step = sem("cond_step")
        condT_ps = sem("condT_ps")
        condT_done = sem("condT_done")
        mod_ps = sem("mod_ps")
        mod_step = sem("mod_step")
        mod_stored = sem("mod_stored")
        w_hi = sem("w_hi")
        w_lo = sem("w_lo")
        w_rot = sem("w_rot")
        stacks_clear = sem("stacks_clear")
        selector = sem("selector")

        x_loaded = sem("x_loaded")
        x_copied = sem("x_copied")
        mod1_loaded = sem("mod1_loaded")
        mod2_loaded = sem("mod2_loaded")
        mod3_loaded = sem("mod3_loaded")
        ln1_stats = sem("ln1_stats")
        ln1_var = sem("ln1_var")
        ln1_rstd = sem("ln1_rstd")
        ln1_factor = sem("ln1_factor")
        ln1_done = sem("ln1_done")
        ln1_hi = sem("ln1_hi")
        ln1_lo = sem("ln1_lo")
        ln2_stats = sem("ln2_stats")
        ln2_var = sem("ln2_var")
        ln2_rstd = sem("ln2_rstd")
        ln2_factor = sem("ln2_factor")
        ln2_done = sem("ln2_done")
        ln2_hi = sem("ln2_hi")
        ln2_lo = sem("ln2_lo")
        turned = sem("turned")
        turn_part = sem("turn_part")
        turn_out = sem("turn_out")
        qk_ps = sem("qk_ps")
        rope_half = sem("rope_half")
        rope_sum = sem("rope_sum")
        qk_hi = sem("qk_hi")
        qk_lo = sem("qk_lo")
        v_ps = sem("v_ps")
        v_hi = sem("v_hi")
        v_lo = sem("v_lo")
        q_stacked = sem("q_stacked")
        k_stacked = sem("k_stacked")
        v_stacked = sem("v_stacked")
        s_ps = sem("s_ps")
        smax_done = sem("smax_done")
        smaxT_ps = sem("smaxT_ps")
        smaxT_done = sem("smaxT_done")
        smax_stacked = sem("smax_stacked")
        st_ps = sem("st_ps")
        exp_done = sem("exp_done")
        p_hi = sem("p_hi")
        p_lo = sem("p_lo")
        pv_ps = sem("pv_ps")
        rsum_done = sem("rsum_done")
        o_done = sem("o_done")
        o_hi = sem("o_hi")
        o_lo = sem("o_lo")
        attn_ps = sem("attn_ps")
        gated1 = sem("gated1")
        mid_done = sem("mid_done")
        h_ps = sem("h_ps")
        gelu_done = sem("gelu_done")
        h_hi = sem("h_hi")
        h_lo = sem("h_lo")
        mlp_ps = sem("mlp_ps")
        gated2 = sem("gated2")
        out_done = sem("out_done")
        stored = sem("stored")

        block = ctx.enter_context(nc.Block())

        def turn_count(i):
            return 0 if isinstance(i, int) and i == 0 else i * (3 * T) - T

        @block.sync
        def _(sp):
            sp.dma_start(cond_sb, cond).then_inc(cond_in, 16)
            sp.dma_start(stage_ada, ada_w.rearrange("(k p) n -> p k n", p=P)).then_inc(ada_in, 16)
            sp.dma_start(ada_b_sb.rearrange("p s n -> p (s n)"), ada_b.partition_broadcast(P)).then_inc(ada_in, 16)
            for n, v in enumerate((g1, b1, g2, b2)):
                sp.dma_start(stage_norm[:, n, :], v.partition_broadcast(P)).then_inc(ada_in, 16)
            for n, w in enumerate((wq, wk, wv, wo)):
                sp.dma_start(stage_qkvo[:, n], w.rearrange("(k p) n -> p k n", p=P)).then_inc(wqkvo_in, 16)
            sp.dma_start(table[:], rope).then_inc(rope_in, 16)
            sp.dma_start(x_in[:].rearrange("p t c -> p (t c)"), x_g[0]).then_inc(x_loaded, 16)
            sp.dma_start(stage_w1, w1.rearrange("(k p) n -> p k n", p=P)).then_inc(wmlp_in, 16)
            sp.dma_start(stage_w2, w2.rearrange("(u p) n -> p u n", p=P)).then_inc(wmlp_in, 16)
            sp.wait_ge(mod_step, 15)
            sp.dma_start(mod_dram, mod_out).then_inc(mod_stored, 16)
            sp.wait_ge(mod_stored, 16)

            def load_mod(dst, g, s0, s1, done):
                sp.wait_ge(mod_stored, 16)
                src = mod_g[g][:, s0:s1, :].rearrange("b s c -> b (s c)")
                rows = src.unsqueeze(1).to_broadcast([GB, I, (s1 - s0) * C])
                sp.dma_start(dst.rearrange("p s c -> p (s c)"), rows).then_inc(done, 16)

            def restack(i, mlp):
                for qk, src, stack, done, parts in ((0, q_16, q_stack, q_stacked, (0, 0, 1)),
                                                    (1, k_16, k_stack, k_stacked, (0, 1, 0))):
                    for kt in range(KT):
                        count = i * 8 + 4 * qk + 2 * kt + 2
                        for part in range(2):
                            sp.wait_ge(qk_lo if part else qk_hi, count)
                            if mlp and qk == kt == part == 0:
                                sp.wait_ge(st_ps, i * GB)
                            for c in range(3):
                                if parts[c] != part:
                                    continue
                                for j in range(JK):
                                    sp.dma_start(stack[32 * c:32 * c + 32, JK * kt + j],
                                                 src[32 * j:32 * j + 32, kt, part]).then_inc(done, 16)

            def restack_v(i):
                sp.wait_ge(v_hi, i * BP + BP)
                sp.wait_ge(v_lo, i * BP + BP)
                for a in range(2):
                    for b in range(2):
                        src = v_16[N * b:N * b + N, :, a].rearrange("m q h j e -> m q (h j e)")
                        dst = v_diag[N * a:N * a + N, b:GB:2, a].rearrange("m q h j e -> m q (h j e)")
                        sp.dma_start(dst, src).then_inc(v_stacked, 16)

            def stack_max(i, half):
                sp.wait_ge(smaxT_done, i * BP + 2 * half + 2)
                cols = slice(half * 2 * P, half * 2 * P + 2 * P)
                for a in range(2):
                    src = smaxT[a:H:2, cols]
                    sp.dma_start(q_stack[96 + a:97 + a, :, cols], src).then_inc(smax_stacked, 16)

            def iteration(i, attention, mlp, norm_next):
                if attention:
                    if mlp:
                        sp.wait_ge(mid_done, i * T)
                    sp.wait_ge(x_loaded, i * 16 + 16)
                    sp.dma_start(x_res[:], x_in[:]).then_inc(x_copied, 16)
                if norm_next:
                    sp.wait_ge(ln1_done, i * T + T)
                    sp.wait_ge(x_copied, i * 16 + 16)
                    sp.wait_ge(mod_stored, 16)
                    sp.dma_start(x_in[:].rearrange("p t c -> p (t c)"), x_g[i + 1]).then_inc(x_loaded, 16)
                    load_mod(mod1[:], i + 1, 0, 2, mod1_loaded)
                if attention:
                    restack(i, mlp)
                    if mlp:
                        sp.wait_ge(pv_ps, i * BP)
                    restack_v(i)
                    if mlp:
                        sp.wait_ge(ln2_done, i * T)
                    load_mod(mod2[:], i, 2, 5, mod2_loaded)
                    stack_max(i, 0)
                    stack_max(i, 1)
                if mlp:
                    sp.wait_ge(out_done, i * T)
                    sp.wait_ge(mod_stored, 16)
                    sp.dma_start(out_g[i - 1], out_sb[:].rearrange("p t c -> p (t c)")).then_inc(stored, 16)
                if attention:
                    if mlp:
                        sp.wait_ge(gated2, i * T)
                    load_mod(mod3[:], i, 5, 6, mod3_loaded)

            load_mod(mod1[:], 0, 0, 2, mod1_loaded)
            sp.wait_ge(selector, 1)
            sp.wait_ge(stacks_clear, 3)
            iteration(0, True, False, True)
            iteration(1, True, True, True)
            with sp.Fori(2, G - 1) as i:
                iteration(i, True, True, True)
            iteration(G - 1, True, True, False)
            iteration(G, False, True, False)
            sp.wait_ge(stored, 16 * G)

        @block.gpsimd
        def _(pool):
            pool.memset(minus_half[:], -0.5).then_inc(zeroed, 1)
            pool.memset(ident16[:], 0.0).then_inc(zeroed, 1)
            pool.memset(ident32[:], 0.0).then_inc(zeroed, 1)
            pool.wait_ge(zeroed, 3)
            for m in (ident16, ident32):
                pool.affine_select(out=m[:], in_=m[:], compare_op=ALU.not_equal, fill=1.0, base=0,
                                   pattern=[[-1, P]], channel_multiplier=1).then_inc(ident_done, 1)
            pool.memset(v_16[:, :, :, 0, :, D:D1].rearrange("p q a j e -> p (q a) (j e)"), 1.0).then_inc(stacks_clear, 1)
            pool.memset(v_16[:, :, :, 1, :, D:D1].rearrange("p q a j e -> p (q a) (j e)"), 0.0).then_inc(stacks_clear, 1)
            pool.memset(v_diag[:].rearrange("p b a h j e -> p (b a h j e)"), 0.0).then_inc(stacks_clear, 1)
            pool.wait_ge(mod_ps, 3)
            pool.wait_ge(mod_step, 15)
            pool.memset(k_stack[:].rearrange("p j b a n -> p (j b a n)"), 0.0).then_inc(zeroed, 1)
            pool.wait_ge(zeroed, 4)
            k_sel = k_stack[96:98].rearrange("p j b a n -> p (j b) a n")
            pool.affine_select(out=k_sel, in_=k_sel, compare_op=ALU.not_equal, fill=-MAX_SCALE, base=0,
                               pattern=[[0, J * GB], [-1, 2], [0, N]], channel_multiplier=1).then_inc(selector, 1)

            pool.wait_ge(selector, 1)

            def norm_rstd(k, g, var, done):
                pool.wait_ge(var, g + 1)
                pool.tensor_tensor(rstd[:, k], var_eps[:, k], minus_half[:], ALU.pow).then_inc(done, 1)

            def norm_lo(g, n32, n16, hi, lo, used):
                for t in range(T):
                    pool.wait_ge(hi, g * T + t + 1)
                    pool.tensor_tensor(n16[:, t, 1], n32[:, t], n16[:, t, 0], ALU.subtract).then_inc(lo, 1)

            def iteration(i, attention, mlp, norm_next):
                if mlp:
                    for t in range(T):
                        pool.wait_ge(gated1, (i - 1) * T + t + 1)
                        if t == 0:
                            pool.wait_ge(x_copied, i * 16)
                        pool.tensor_tensor(x_mid[:, t], gated[:, t % 2], x_res[:, t], ALU.add).then_inc(mid_done, 1)
                    norm_rstd(1, i - 1, ln2_var, ln2_rstd)
                if attention:
                    for c in range(4):
                        pool.wait_ge(rope_half, i * 8 + 2 * c + 2)
                        if c >= 2:
                            pool.wait_ge(qk_lo, i * 8 + 2 * c - 2)
                        elif mlp:
                            pool.wait_ge(qk_lo, i * 8 + 2 * c - 2)
                        pool.tensor_tensor(qk_32[:, c % 2], rope_c[:, c % 2], rope_s[:, c % 2], ALU.add).then_inc(rope_sum, 1)
                if mlp:
                    norm_lo(i - 1, n2_32, n2_16, ln2_hi, ln2_lo, None)
                if norm_next:
                    norm_rstd(0, i + 1, ln1_var, ln1_rstd)
                    norm_lo(i + 1, n1_32, n1_16, ln1_hi, ln1_lo, None)
                if mlp:
                    for t in range(T):
                        pool.wait_ge(gated2, (i - 1) * T + t + 1)
                        if t == 0 and not (isinstance(i, int) and i == 1):
                            pool.wait_ge(stored, (i - 1) * 16)
                        pool.tensor_tensor(out_sb[:, t], gated[:, t % 2], x_mid[:, t], ALU.add).then_inc(out_done, 1)

            norm_rstd(0, 0, ln1_var, ln1_rstd)
            norm_lo(0, n1_32, n1_16, ln1_hi, ln1_lo, None)
            iteration(0, True, False, True)
            iteration(1, True, True, True)
            with pool.Fori(2, G - 1) as i:
                iteration(i, True, True, True)
            iteration(G - 1, True, True, False)
            iteration(G, False, True, False)

        @block.scalar
        def _(act):
            act.wait_ge(cond_in, 16)
            act.activation(cond_e, cond_sb, ACT.Exp, scale=-1.0).then_inc(cond_exp, 1)
            act.wait_ge(condT_ps, 1)
            act.activation(condT, ps_score[0][:, 0:C].rearrange("p (k b) -> p k b", k=KT), ACT.Copy).then_inc(condT_done, 1)
            act.wait_ge(wqkvo_in, 64)
            for n in range(2):
                act.activation(w_qk[:, 0, 2 * n], stage_qkvo[:, n], ACT.Copy, scale=W_SCALE).then_inc(w_hi, 1)
            for kt in range(KT):
                act.activation(w_v[:, 0, kt].rearrange("p (a j r) -> p a j r", a=2, r=D),
                               stage_qkvo[:, 2, kt].rearrange("p (j a r) -> p a j r", a=2, r=D),
                               ACT.Copy, scale=V_SCALE).then_inc(w_hi, 1)
            act.activation(w_o[:, 0], stage_qkvo[:, 3], ACT.Copy, scale=W_SCALE).then_inc(w_hi, 1)
            act.wait_ge(wmlp_in, 32)
            act.activation(w_1[:, 0], stage_w1, ACT.Copy, scale=W_SCALE).then_inc(w_hi, 1)
            act.activation(w_2[:, 0], stage_w2, ACT.Copy, scale=W_SCALE).then_inc(w_hi, 1)

            def norm_hi(g, n32, n16, done, hi):
                for t in range(T):
                    act.wait_ge(done, g * T + t + 1)
                    act.activation(n16[:, t, 0], n32[:, t], ACT.Copy).then_inc(hi, 1)

            def turn_out_group(base, dst):
                for t in range(T):
                    act.wait_ge(turned, base + t + 1)
                    act.activation(dst(t), ps_turn_view(t), ACT.Copy).then_inc(turn_out, 1)

            def ps_turn_view(t):
                return ps_turn[t % 2].rearrange("p h k n -> p (h k) n")

            def iteration(i, attention, mlp, norm_next):
                base = turn_count(i)
                if attention:
                    def n1T_tile(t):
                        return n1T[:].rearrange("p h k (b t i) -> p (h k) b t i", t=T, i=I)[:, :, :, t]
                    for t in range(T):
                        act.wait_ge(turned, base + t + 1)
                        act.activation(n1T_tile(t), ps_turn[t % 2].rearrange("p h k (b i) -> p (h k) b i", i=I),
                                       ACT.Copy).then_inc(turn_out, 1)
                if attention:
                    for c in range(4):
                        if mlp and c == 1:
                            norm_hi(i - 1, n2_32, n2_16, ln2_done, ln2_hi)
                        act.wait_ge(rope_sum, i * 4 + c + 1)
                        if mlp and c == 0:
                            act.wait_ge(q_stacked, i * (16 * 3 * J))
                            act.wait_ge(k_stacked, i * (16 * 3 * J))
                        if c < 2:
                            act.activation(q_16[:, c, 0], qk_32[:, c % 2], ACT.Copy).then_inc(qk_hi, 2)
                        else:
                            for a in range(2):
                                act.activation(k_16[:, c - 2, 0, :, a],
                                               qk_32[:, c % 2].rearrange("p (b n) -> p b n", n=N),
                                               ACT.Identity, scale=parity[:, a:a + 1]).then_inc(qk_hi, 1)
                    for q in range(BP):
                        act.wait_ge(v_ps, i * BP + q + 1)
                        if q == 0 and mlp:
                            act.wait_ge(v_stacked, i * 64)
                        act.activation(v_16[:, q, :, 0, :, 0:D], ps_tok[q % 2].rearrange("p (a j r) -> p a j r", a=2, r=D),
                                       ACT.Copy).then_inc(v_hi, 1)
                if mlp and not attention:
                    norm_hi(i - 1, n2_32, n2_16, ln2_done, ln2_hi)
                if mlp:
                    turn_out_group(base + T if attention else base,
                                   lambda t: n2T[:, :, :, t * P:t * P + P].rearrange("p h k n -> p (h k) n"))
                    for u in range(FU):
                        act.wait_ge(h_ps, (i - 1) * FU + u + 1)
                        if u >= 2 or not (isinstance(i, int) and i == 1):
                            act.wait_ge(h_lo, (i - 1) * FU + u - 1)
                        act.activation(h_32[:, u % 2], ps_proj[u % 2][:], ACT.Gelu, scale=GELU_SCALE).then_inc(gelu_done, 1)
                        act.wait_ge(gelu_done, (i - 1) * FU + u + 1)
                        if u == 0 and not (isinstance(i, int) and i == 1):
                            act.wait_ge(mlp_ps, (i - 1) * T)
                        act.activation(h_16[:, u, 0], h_32[:, u % 2], ACT.Copy).then_inc(h_hi, 1)
                if attention:
                    for q in range(BP):
                        act.wait_ge(smaxT_ps, i * BP + q + 1)
                        if q == 0 and mlp:
                            act.wait_ge(smax_stacked, i * 64)
                        act.activation(smaxT[:, q * P:q * P + P], ps_smaxT[q % 2], ACT.Copy,
                                       scale=1.0 / MAX_SCALE).then_inc(smaxT_done, 1)

                    def softmax(b):
                        act.wait_ge(st_ps, i * GB + b + 1)
                        if b >= 2 or mlp:
                            act.wait_ge(p_lo, i * GB + b - 1)
                        act.activation(p_32[:, b % 2], ps_score[b % 2][:], ACT.Exp, scale=EXP_SCALE).then_inc(exp_done, 1)
                        act.wait_ge(exp_done, i * GB + b + 1)
                        if b % 2 == 0 and (b >= 4 or mlp):
                            act.wait_ge(pv_ps, i * BP + b // 2 - 1)
                        act.activation(p_16[:, b % 4, 0], p_32[:, b % 2], ACT.Copy).then_inc(p_hi, 1)

                    def o_high(q):
                        act.wait_ge(o_done, i * BP + q + 1)
                        if q == 0 and mlp:
                            act.wait_ge(turned, base)
                        act.activation(o_16[:, q, 0], o_32[:, q % 2], ACT.Copy).then_inc(o_hi, 1)

                    for b in range(GB):
                        softmax(b)
                        if b == 3 and norm_next:
                            norm_hi(i + 1, n1_32, n1_16, ln1_done, ln1_hi)
                        if b % 2 == 1 and b >= 3:
                            o_high(b // 2 - 1)
                    o_high(BP - 1)
                    base_o = base + (2 * T if mlp else T)
                    for q in range(BP):
                        act.wait_ge(turned, base_o + q + 1)
                        for b in range(2):
                            src = ps_turn[q % 2].rearrange("p h k (b t i) -> p (h k) b t i", b=2, i=I)[:, :, b]
                            dst = oT[:].rearrange("p h k (t b i) -> p (h k) b t i", t=T, i=I)[:, :, 2 * q + b]
                            ins = act.activation(dst, src, ACT.Copy)
                            if b == 0:
                                ins.then_inc(turn_part, 1)
                        ins.then_inc(turn_out, 1)

            norm_hi(0, n1_32, n1_16, ln1_done, ln1_hi)
            iteration(0, True, False, True)
            iteration(1, True, True, True)
            with act.Fori(2, G - 1) as i:
                iteration(i, True, True, True)
            iteration(G - 1, True, True, False)
            iteration(G, False, True, False)

        @block.vector
        def _(dve):
            dve.wait_ge(cond_exp, 1)
            dve.tensor_scalar(cond_e, cond_e, 1.0, None, ALU.add).then_inc(cond_step, 1)
            dve.wait_ge(cond_step, 1)
            dve.reciprocal(cond_r, cond_e).then_inc(cond_step, 1)
            dve.wait_ge(cond_step, 2)
            dve.tensor_tensor(cond_s, cond_sb, cond_r, ALU.mult).then_inc(cond_step, 1)

            def norm_stats(k, g, src, in_done, in_count, stats_done, var_done):
                for t in range(T):
                    if t in in_count:
                        for s, v in in_count[t]:
                            dve.wait_ge(s, v)
                    dve.bn_stats(stats[:, k, t], src[:, t]).then_inc(stats_done, 1)
                dve.wait_ge(stats_done, g * (2 * T + 1) + T)
                dve.memset(var_eps[:, k], EPS).then_inc(stats_done, 1)
                for t in range(T):
                    dve.bn_aggr(moments[:, k, t], stats[:, k, t]).then_inc(stats_done, 1)
                dve.wait_ge(stats_done, g * (2 * T + 1) + 2 * T + 1)
                dve.tensor_tensor(var_eps[:, k], moments[:, k, :, 1], var_eps[:, k], ALU.add).then_inc(var_done, 1)

            def norm_apply(k, g, src, mod, m0, n32, factor, rstd_done, done, free):
                for t in range(T):
                    if t == 0:
                        for s, v in free:
                            dve.wait_ge(s, v)
                    dve.scalar_tensor_tensor(n32[:, t], src[:, t], moments[:, k, t, 0:1], mod[:, m0],
                                             ALU.subtract, ALU.mult).then_inc(factor, 1)
                dve.wait_ge(rstd_done, g + 1)
                for t in range(T):
                    dve.wait_ge(factor, g * T + t + 1)
                    dve.scalar_tensor_tensor(n32[:, t], n32[:, t], rstd[:, k, t:t + 1], mod[:, m0 + 1],
                                             ALU.mult, ALU.add).then_inc(done, 1)

            def norm1(g):
                first = isinstance(g, int) and g == 0
                norm_stats(0, g, x_in, None, {0: [(x_loaded, g * 16 + 16)]}, ln1_stats, ln1_var)
                norm_apply(0, g, x_in, mod1, 0, n1_32, ln1_factor, ln1_rstd, ln1_done,
                           [(mod1_loaded, g * 16 + 16)] + ([] if first else [(ln1_lo, g * T)]))

            dve.wait_ge(ada_in, 16 * 6)
            for n, ps in enumerate((ps_proj[0], ps_proj[1], ps_score[1])):
                dve.wait_ge(mod_ps, n + 1)
                dve.tensor_tensor(stage_mod[:, 2 * n:2 * n + 2] if n < 2 else stage_mod2, ps[:].rearrange("p (s c) -> p s c", s=2),
                                  ada_b_sb[:, 2 * n:2 * n + 2], ALU.add).then_inc(mod_step, 1)
            dve.wait_ge(mod_step, 3)
            for n, (fac, sh) in enumerate(((0, 1), (3, 4))):
                scale, shift = mod_row(3 * n + 1), mod_row(3 * n)
                dve.scalar_tensor_tensor(mod_out[:, fac], scale, 1.0, stage_norm[:, 2 * n], ALU.add, ALU.mult).then_inc(mod_step, 1)
                dve.scalar_tensor_tensor(mod_out[:, sh], scale, 1.0, stage_norm[:, 2 * n + 1], ALU.add, ALU.mult).then_inc(mod_step, 1)
                dve.wait_ge(mod_step, 3 + 5 * n + 2)
                dve.tensor_tensor(mod_out[:, sh], mod_out[:, sh], shift, ALU.add).then_inc(mod_step, 1)
                dve.wait_ge(mod_step, 3 + 5 * n + 3)
                for m in (fac, sh):
                    dve.tensor_scalar(mod_out[:, m], mod_out[:, m], X_SCALE, None, ALU.mult).then_inc(mod_step, 1)
            dve.tensor_scalar(mod_out[:, 2], mod_row(2), GATE1_SCALE, None, ALU.mult).then_inc(mod_step, 1)
            dve.tensor_scalar(mod_out[:, 5], mod_row(5), GATE2_SCALE, None, ALU.mult).then_inc(mod_step, 1)

            def low(dst, src, hi, scale, count):
                dve.wait_ge(w_hi, count)
                dve.scalar_tensor_tensor(dst, src, scale, hi, ALU.mult, ALU.subtract).then_inc(w_lo, 1)

            count = 0
            for n in range(2):
                count += 1
                low(w_qk[:, 1, 2 * n], stage_qkvo[:, n], w_qk[:, 0, 2 * n], W_SCALE, count)
            for kt in range(KT):
                count += 1
                for a in range(2):
                    low(w_v[:, 1, kt].rearrange("p (a j r) -> p a j r", a=2, r=D)[:, a],
                        stage_qkvo[:, 2, kt].rearrange("p (j a r) -> p a j r", a=2, r=D)[:, a],
                        w_v[:, 0, kt].rearrange("p (a j r) -> p a j r", a=2, r=D)[:, a], V_SCALE, count)
            for dst, src in ((w_o, stage_qkvo[:, 3]), (w_1, stage_w1), (w_2, stage_w2)):
                count += 1
                low(dst[:, 1], src, dst[:, 0], W_SCALE, count)
                if dst is w_o:
                    dve.wait_ge(w_lo, 7)
                    for n in range(2):
                        for part in range(2):
                            plain = w_qk[:, part, 2 * n].rearrange("p k (h r) -> p (k h) r", r=D)
                            turnd = w_qk[:, part, 2 * n + 1].rearrange("p k (h r) -> p (k h) r", r=D)
                            dve.tensor_copy(turnd[:, :, 0:D // 2], plain[:, :, 1:D:2]).then_inc(w_rot, 1)
                            dve.tensor_copy(turnd[:, :, D // 2:D], plain[:, :, 0:D:2]).then_inc(w_rot, 1)
                    norm1(0)
            dve.wait_ge(rope_in, 16)

            def rotary_unit(i, u, mlp):
                c = u // 2
                dve.wait_ge(qk_ps, i * 8 + u + 1)
                if c >= 2:
                    dve.wait_ge(rope_sum, i * 4 + c - 1)
                elif mlp:
                    dve.wait_ge(rope_sum, i * 4 + c - 1)
                dst = (rope_c if u % 2 == 0 else rope_s)[:, c % 2].rearrange("p (b n) -> p b n", b=GB)
                dve.tensor_tensor(dst, ps_proj[u % 2][:].rearrange("p (b n) -> p b n", b=GB),
                                  rope_sb[:, u % 2].unsqueeze(1).to_broadcast([P, GB, N]), ALU.mult).then_inc(rope_half, 1)

            def qk_low(i, c):
                dve.wait_ge(qk_hi, i * 8 + 2 * c + 2)
                if c < 2:
                    dve.tensor_tensor(q_16[:, c, 1], qk_32[:, c % 2], q_16[:, c, 0], ALU.subtract).then_inc(qk_lo, 2)
                    return
                for a in range(2):
                    dve.scalar_tensor_tensor(k_16[:, c - 2, 1, :, a], qk_32[:, c % 2].rearrange("p (b n) -> p b n", n=N),
                                             parity[:, a:a + 1], k_16[:, c - 2, 0, :, a], ALU.mult,
                                             ALU.subtract).then_inc(qk_lo, 1)

            def v_low(i, q):
                dve.wait_ge(v_hi, i * BP + q + 1)
                dve.tensor_tensor(v_16[:, q, :, 1, :, 0:D], ps_tok[q % 2].rearrange("p (a j r) -> p a j r", a=2, r=D),
                                  v_16[:, q, :, 0, :, 0:D], ALU.subtract).then_inc(v_lo, 1)

            def h_low(g, u):
                dve.wait_ge(h_hi, g * FU + u + 1)
                dve.tensor_tensor(h_16[:, u, 1], h_32[:, u % 2], h_16[:, u, 0], ALU.subtract).then_inc(h_lo, 1)

            def score_max(i, s):
                dve.wait_ge(s_ps, i * 8 + s + 1)
                dve.tensor_reduce(smax[:, s // 2, J * (s % 2):J * (s % 2) + J],
                                  ps_score[s % 2][:].rearrange("p (h m) -> p h m", m=N), AX_X, ALU.max).then_inc(smax_done, 1)

            def p_low(i, b):
                dve.wait_ge(p_hi, i * GB + b + 1)
                dve.tensor_tensor(p_16[:, b % 4, 1], p_32[:, b % 2], p_16[:, b % 4, 0], ALU.subtract).then_inc(p_lo, 1)

            def attn_out(i, q, mlp):
                pv = pv_out[q % 2]
                dve.wait_ge(pv_ps, i * BP + q + 1)
                dve.reciprocal(rsum[:, q], pv[:, :, D]).then_inc(rsum_done, 1)
                dve.wait_ge(rsum_done, i * BP + q + 1)
                if q >= 2 or mlp:
                    dve.wait_ge(o_lo, i * BP + q - 1)
                dve.tensor_tensor(o_32[:, q % 2].rearrange("p (h r) -> p h r", r=D), pv[:, :, 0:D],
                                  rsum[:, q].unsqueeze(2).to_broadcast([P, H, D]), ALU.mult).then_inc(o_done, 1)

            def o_low(i, q):
                dve.wait_ge(o_hi, i * BP + q + 1)
                dve.tensor_tensor(o_16[:, q, 1], o_32[:, q % 2], o_16[:, q, 0], ALU.subtract).then_inc(o_lo, 1)

            def gate_2(g, t):
                dve.wait_ge(mlp_ps, g * T + t + 1)
                if t == 0:
                    dve.wait_ge(mod3_loaded, g * 16 + 16)
                    dve.wait_ge(mid_done, g * T + T)
                if t >= 2:
                    dve.wait_ge(out_done, g * T + t - 1)
                dve.tensor_tensor(gated[:, t % 2], ps_tok[t % 2], mod3[:, 0], ALU.mult).then_inc(gated2, 1)

            def iteration(i, attention, mlp, norm_next):
                if mlp:
                    for t in range(T):
                        dve.wait_ge(attn_ps, (i - 1) * T + t + 1)
                        if t == 0:
                            dve.wait_ge(mod2_loaded, i * 16)
                            dve.wait_ge(out_done, (i - 2) * T + T) if not isinstance(i, int) or i >= 2 else None
                        if t >= 2:
                            dve.wait_ge(mid_done, (i - 1) * T + t - 1)
                        dve.tensor_tensor(gated[:, t % 2], ps_tok[t % 2], mod2[:, 0], ALU.mult).then_inc(gated1, 1)
                if attention:
                    rotary_unit(i, 0, mlp)
                    rotary_unit(i, 1, mlp)
                if mlp:
                    norm_stats(1, i - 1, x_mid, None, {t: [(mid_done, (i - 1) * T + t + 1)] for t in range(T)}, ln2_stats, ln2_var)
                if attention:
                    rotary_unit(i, 2, mlp)
                    rotary_unit(i, 3, mlp)
                    qk_low(i, 0)
                if mlp:
                    norm_apply(1, i - 1, x_mid, mod2, 1, n2_32, ln2_factor, ln2_rstd, ln2_done,
                               [] if isinstance(i, int) and i == 1 else [(ln2_lo, (i - 1) * T)])
                if attention:
                    rotary_unit(i, 4, mlp)
                    rotary_unit(i, 5, mlp)
                    qk_low(i, 1)
                    rotary_unit(i, 6, mlp)
                    rotary_unit(i, 7, mlp)
                    qk_low(i, 2)
                    qk_low(i, 3)
                    for q in range(BP):
                        v_low(i, q)
                for u in range(FU // 2):
                    if mlp:
                        h_low(i - 1, u)
                for s in range(8):
                    if attention:
                        score_max(i, s)
                    if mlp and s % 2 == 1:
                        h_low(i - 1, FU // 2 + s // 2)
                if norm_next:
                    norm1(i + 1)
                if mlp:
                    gate_2(i - 1, 0)
                if attention:
                    p_low(i, 0)
                    p_low(i, 1)
                if mlp:
                    gate_2(i - 1, 1)
                if attention:
                    p_low(i, 2)
                    p_low(i, 3)
                    attn_out(i, 0, mlp)
                    o_low(i, 0)
                if mlp:
                    gate_2(i - 1, 2)
                if attention:
                    p_low(i, 4)
                    p_low(i, 5)
                    attn_out(i, 1, mlp)
                    o_low(i, 1)
                    p_low(i, 6)
                    p_low(i, 7)
                    attn_out(i, 2, mlp)
                    o_low(i, 2)
                    attn_out(i, 3, mlp)
                    o_low(i, 3)
                if mlp:
                    gate_2(i - 1, 3)

            iteration(0, True, False, True)
            iteration(1, True, True, True)
            with dve.Fori(2, G - 1) as i:
                iteration(i, True, True, True)
            iteration(G - 1, True, True, False)
            iteration(G, False, True, False)

        @block.tensor
        def _(pe):
            PARTS = ((0, 0), (0, 1), (1, 0))

            pe.wait_ge(ident_done, 2)
            pe.wait_ge(cond_step, 3)
            for kt in range(KT):
                mm = pe.transpose(ps_score[0][:, kt * P:kt * P + P], cond_s[:, kt * P:kt * P + P], ident32[:])
            mm.then_inc(condT_ps, 1)
            pe.wait_ge(condT_done, 1)
            pe.wait_ge(ada_in, 16 * 6)
            for n, ps in enumerate((ps_proj[0], ps_proj[1], ps_score[1])):
                for kt in range(KT):
                    mm = pe.matmul(ps[:], condT[:, kt], stage_ada[:, kt, n * 512:n * 512 + 512],
                                   start=(kt == 0), stop=(kt == KT - 1))
                mm.then_inc(mod_ps, 1)
            pe.wait_ge(mod_step, 3)
            pe.wait_ge(w_lo, 9)
            pe.wait_ge(w_rot, 8)

            def turn(use, t, src, first):
                if not first:
                    pe.wait_ge(turn_out, use + t - 1)
                for part in range(2):
                    for kt in range(KT):
                        mm = pe.transpose(ps_turn[t % 2][:, part, kt], src[:, part, kt * P:kt * P + P], ident16[:])
                mm.then_inc(turned, 1)

            def qk_unit(i, u, mlp):
                c, rot = u // 2, u % 2
                if u >= 2:
                    pe.wait_ge(rope_half, i * 8 + u - 1)
                elif mlp and u == 0 and not (isinstance(i, int) and i == 1):
                    pe.wait_ge(gelu_done, (i - 1) * FU)
                w = w_qk[:, :, 2 * (c // 2) + rot, :, (c % 2) * P:(c % 2) * P + P]
                for n, (a, b) in enumerate(PARTS):
                    for kt in range(KT):
                        mm = pe.matmul(ps_proj[u % 2][:], w[:, a, kt], n1T[:, b, kt],
                                       start=(n == 0 and kt == 0), stop=(n == 2 and kt == KT - 1))
                mm.then_inc(qk_ps, 1)

            def v_unit(i, q, mlp):
                if q >= 2:
                    pe.wait_ge(v_hi, i * BP + q - 1)
                    pe.wait_ge(v_lo, i * BP + q - 1)
                elif mlp and q == 0:
                    pe.wait_ge(gated1, i * T)
                for n, (a, b) in enumerate(PARTS):
                    for kt in range(KT):
                        mm = pe.matmul(ps_tok[q % 2], n1T[:, a, kt, q * P:q * P + P], w_v[:, b, kt],
                                       start=(n == 0 and kt == 0), stop=(n == 2 and kt == KT - 1))
                mm.then_inc(v_ps, 1)

            def mlp1_unit(g, u, attention):
                if u >= 2:
                    pe.wait_ge(gelu_done, g * FU + u - 1)
                elif u == 0:
                    if attention:
                        pe.wait_ge(rope_half, (g + 2) * 8)
                    pe.wait_ge(turn_out, turn_count(g + 1) + (2 * T if attention else T))
                for n, (a, b) in enumerate(PARTS):
                    for kt in range(KT):
                        mm = pe.matmul(ps_proj[u % 2][:], w_1[:, a, kt, u * P:u * P + P], n2T[:, b, kt],
                                       start=(n == 0 and kt == 0), stop=(n == 2 and kt == KT - 1))
                mm.then_inc(h_ps, 1)

            def mlp2_part(g, t, half, attention):
                if half == 0:
                    if t >= 2:
                        pe.wait_ge(gated2, g * T + t - 1)
                    elif t == 0 and attention:
                        pe.wait_ge(v_lo, (g + 2) * BP)
                    if t == 0:
                        pe.wait_ge(h_hi, g * FU + FU)
                        pe.wait_ge(h_lo, g * FU + FU)
                for u in range(half * FU // 2, (half + 1) * FU // 2):
                    for n, (a, b) in enumerate(PARTS):
                        mm = pe.matmul(ps_tok[t % 2], h_16[:, u, a, t * P:t * P + P], w_2[:, b, u],
                                       start=(u == 0 and n == 0), stop=(u == FU - 1 and n == 2))
                if half == 1:
                    mm.then_inc(mlp_ps, 1)

            def score_unit(i, s, mlp):
                q, half = s // 2, s % 2
                if s >= 2:
                    pe.wait_ge(smax_done, i * 8 + s - 1)
                elif s == 0:
                    if mlp:
                        pe.wait_ge(exp_done, i * GB)
                    pe.wait_ge(q_stacked, (i + 1) * (16 * 3 * J))
                    pe.wait_ge(k_stacked, (i + 1) * (16 * 3 * J))
                for j in range(JK):
                    for b in range(2):
                        jj, cols = JK * half + j, slice(N * (2 * q + b), N * (2 * q + b) + N)
                        mm = pe.matmul(ps_score[s % 2][N * b:N * b + N, 2 * N * j:2 * N * j + 2 * N],
                                       q_stack[0:96, jj, cols], k_stack[0:96, jj, 2 * q + b].rearrange("p a n -> p (a n)"), start=True, stop=True)
                mm.then_inc(s_ps, 1)

            def max_turn(i, q, mlp):
                pe.wait_ge(smax_done, i * 8 + 2 * q + 2)
                if q >= 2:
                    pe.wait_ge(smaxT_done, i * BP + q - 1)
                elif mlp and q == 0:
                    pe.wait_ge(o_done, i * BP)
                pe.transpose(ps_smaxT[q % 2], smax[:, q], ident32[:]).then_inc(smaxT_ps, 1)

            def softmax_unit(i, b, mlp):
                if b >= 2:
                    pe.wait_ge(exp_done, i * GB + b - 1)
                elif b == 0:
                    pe.wait_ge(smax_done, i * 8 + 8)
                if b % 4 == 0:
                    pe.wait_ge(smax_stacked, i * 64 + (64 if b else 64))
                cols = slice(N * b, N * b + N)
                for j in range(J):
                    mm = pe.matmul(ps_score[b % 2][:, N * j:N * j + N], k_stack[0:98, j, b].rearrange("p a n -> p (a n)"),
                                   q_stack[0:98, j, cols], start=True, stop=True)
                mm.then_inc(st_ps, 1)

            def pv_unit(i, q, mlp):
                pe.wait_ge(p_lo, i * GB + 2 * q + 2)
                pe.wait_ge(p_hi, i * GB + 2 * q + 2)
                if q >= 2:
                    pe.wait_ge(o_done, i * BP + q - 1)
                elif q == 0:
                    pe.wait_ge(v_stacked, i * 64 + 64)
                    pe.wait_ge(smaxT_done, i * BP + BP)
                for b in range(2):
                    for j in range(J):
                        for n, (a, c) in enumerate(PARTS):
                            mm = pe.matmul(pv_out[q % 2][N * b:N * b + N, 2 * j:2 * j + 2, :],
                                           p_16[:, (2 * q + b) % 4, a, N * j:N * j + N],
                                           v_diag[:, 2 * q + b, :, c, j, :], start=(n == 0), stop=(n == 2))
                mm.then_inc(pv_ps, 1)

            def wo_unit(i, t, base_o, mlp):
                if t == 0:
                    pe.wait_ge(turn_out, base_o + T)
                    if mlp:
                        pe.wait_ge(gated2, i * T)
                    else:
                        pe.wait_ge(v_lo, i * BP + BP)
                elif t >= 2:
                    pe.wait_ge(gated1, i * T + t - 1)
                for n, (a, b) in enumerate(PARTS):
                    for kt in range(KT):
                        mm = pe.matmul(ps_tok[t % 2], oT[:, a, kt, t * P:t * P + P], w_o[:, b, kt],
                                       start=(n == 0 and kt == 0), stop=(n == 2 and kt == KT - 1))
                mm.then_inc(attn_ps, 1)

            def iteration(i, attention, mlp, norm_next):
                base = turn_count(i)
                if attention:
                    for t in range(T):
                        pe.wait_ge(ln1_lo, i * T + t + 1)
                        turn(base, t, n1_16[:, t], not mlp and t < 2)
                    pe.wait_ge(turn_out, base + T)
                    for u in range(8):
                        qk_unit(i, u, mlp)
                    for q in range(BP):
                        v_unit(i, q, mlp)
                if mlp:
                    for t in range(T):
                        pe.wait_ge(ln2_lo, (i - 1) * T + t + 1)
                        turn(base + T if attention else base, t, n2_16[:, t], False)
                    for u in range(FU // 2):
                        mlp1_unit(i - 1, u, attention)
                for u in range(4):
                    if attention:
                        score_unit(i, 2 * u, mlp)
                        score_unit(i, 2 * u + 1, mlp)
                    if mlp:
                        mlp1_unit(i - 1, FU // 2 + u, attention)
                if attention:
                    for q in range(BP):
                        max_turn(i, q, mlp)

                def mlp2(t, half):
                    if mlp:
                        mlp2_part(i - 1, t, half, attention)

                def soft(b):
                    if attention:
                        softmax_unit(i, b, mlp)

                def pv(q):
                    if attention:
                        pv_unit(i, q, mlp)

                mlp2(0, 0)
                mlp2(0, 1)
                soft(0)
                soft(1)
                mlp2(1, 0)
                mlp2(1, 1)
                soft(2)
                soft(3)
                pv(0)
                mlp2(2, 0)
                soft(4)
                soft(5)
                mlp2(2, 1)
                pv(1)
                soft(6)
                soft(7)
                pv(2)
                mlp2(3, 0)
                pv(3)
                if attention:
                    base_o = base + (2 * T if mlp else T)
                    for q in range(BP - 1):
                        pe.wait_ge(o_lo, i * BP + q + 1)
                        turn(base_o, q, o_16[:, q], False)
                mlp2(3, 1)
                if attention:
                    pe.wait_ge(o_lo, i * BP + BP)
                    turn(base_o, BP - 1, o_16[:, BP - 1], False)
                    for t in range(T):
                        wo_unit(i, t, base_o, mlp)

            iteration(0, True, False, True)
            iteration(1, True, True, True)
            with pe.Fori(2, G - 1) as i:
                iteration(i, True, True, True)
            iteration(G - 1, True, True, False)
            iteration(G, False, True, False)


_INS = ['x', 'cond_1024', 'L0_cond_norm1_g', 'L0_cond_norm1_b', 'L0_cond_Wq', 'L0_cond_Wk', 'L0_cond_Wv',
        'L0_cond_Wo', 'L0_cond_norm2_g', 'L0_cond_norm2_b', 'L0_cond_W1', 'L0_cond_W2', 'L0_cond_ada_W',
        'L0_cond_ada_b']


def rope_table():
    dim = np.arange(P) % D
    inv_freq = (1.0 / 10000.0 ** (np.arange(0, D, 2, dtype=np.float32) / D)).astype(np.float32)
    t, i = np.meshgrid(np.arange(T), np.arange(I), indexing="ij")
    pos = (T * i + t).reshape(-1).astype(np.float32)
    angle = (pos[None, :] * inv_freq[dim % (D // 2)][:, None]).astype(np.float32)
    sign = np.where(dim < D // 2, -1.0, 1.0).astype(np.float32)[:, None]
    table = np.stack([np.cos(angle), sign * np.sin(angle)], axis=1) * ROPE_SCALE
    head = np.arange(P) // D
    parity = np.stack([head % 2 == 0, head % 2 == 1], axis=1)
    return np.ascontiguousarray(np.concatenate([table.reshape(P, 2 * N), parity], axis=1).astype(np.float32))


def kernel(**inputs):
    import concourse.bacc as _bacc
    from concourse import mybir as _mybir
    from concourse.bass_utils import run_bass_kernel_spmd as _run

    nc = _bacc.Bacc("TRN2", target_bir_lowering=False, num_devices=1)
    arrays, args = {}, []
    for name in _INS + ["rope"]:
        a = rope_table() if name == "rope" else np.ascontiguousarray(inputs[name])
        arrays[f"in_{name}_dram"] = a
        args.append(nc.dram_tensor(f"in_{name}_dram", a.shape, _mybir.dt.from_np(a.dtype), kind="ExternalInput").ap())
    args.append(nc.dram_tensor("out_0_dram", (B, N, C), F32, kind="ExternalOutput").ap())
    build(nc, *args)
    r = _run(nc, [arrays], core_ids=[0])
    return r.results[0]["out_0_dram"]
```

```python
from contextlib import ExitStack

import numpy as np

import concourse.bass as bass
from concourse import mybir

F32 = mybir.dt.float32
F16 = mybir.dt.float16
ALU = mybir.AluOpType
ACT = mybir.ActivationFunctionType
AX_X = mybir.AxisListType.X

P = 128
B, N, C = 128, 64, 256
H, D = 16, 16
F = 4 * C
KT = C // P
GB = 8
G = B // GB
T = 4
I = P // GB
GT = GB * N
J = H // 2
JK = J // KT
BP = GB // 2
FU = F // P
D1 = D + 1
EPS = 1e-5

W_SCALE = 64.0
V_SCALE = 4.0
X_SCALE = 16.0
QK_SCALE = 4.0
ROPE_SCALE = QK_SCALE / (W_SCALE * X_SCALE)
EXP_SCALE = D ** -0.5 / (QK_SCALE * QK_SCALE)
MAX_SCALE = QK_SCALE * QK_SCALE
O_SCALE = V_SCALE * X_SCALE
GATE1_SCALE = 1.0 / (O_SCALE * W_SCALE)
GATE2_SCALE = 1.0 / W_SCALE
GELU_SCALE = 1.0 / (W_SCALE * X_SCALE)


def build(nc, x, cond, g1, b1, wq, wk, wv, wo, g2, b2, w1, w2, ada_w, ada_b, rope, out):
    ctx = ExitStack()
    with ctx:
        def sb(name, shape, dt):
            return ctx.enter_context(nc.sbuf_tensor(name, shape, dt))

        def psum(name, shape, dt):
            return ctx.enter_context(nc.psum_tensor(name, shape, dt))

        def sem(name):
            return ctx.enter_context(nc.semaphore(name))

        x_g = x.rearrange("(g b) (i t) c -> g (b i) (t c)", b=GB, t=T)
        out_g = out.rearrange("(g b) (i t) c -> g (b i) (t c)", b=GB, t=T)
        mod_dram = nc.dram_tensor("mod_scratch", (B, 6, C), F32).ap()
        mod_g = mod_dram.rearrange("(g b) s c -> g b s c", b=GB)

        w_qk = sb("w_qk", [P, 2, 4, KT, C], F16)
        w_v = sb("w_v", [P, 2, KT, C], F16)
        w_o = sb("w_o", [P, 2, KT, C], F16)
        w_1 = sb("w_1", [P, 2, KT, F], F16)
        w_2 = sb("w_2", [P, 2, FU, C], F16)
        ident16 = sb("ident16", [P, P], F16)
        ident32 = sb("ident32", [P, P], F32)
        table = sb("table", [P, 2 * N + 2], F32)
        rope_sb = table[:, 0:2 * N].rearrange("p (s n) -> p s n", s=2)
        parity = table[:, 2 * N:2 * N + 2]
        minus_half = sb("minus_half", [P, T], F32)

        x_in = sb("x_in", [P, T, C], F32)
        x_res = sb("x_res", [P, T, C], F32)
        x_mid = sb("x_mid", [P, T, C], F32)
        x_late = sb("x_late", [P, T, C], F32)
        out_sb = sb("out_sb", [P, T, C], F32)
        mod1 = sb("mod1", [P, 2, C], F32)
        mod2 = sb("mod2", [P, 3, C], F32)
        mod3 = sb("mod3", [P, 1, C], F32)
        stats = sb("stats", [P, 2, T, 6], F32)
        moments = sb("moments", [P, 2, T, 2], F32)
        var_eps = sb("var_eps", [P, 2, T], F32)
        rstd = sb("rstd", [P, 2, T], F32)
        n1_32 = sb("n1_32", [P, T, C], F32)
        n1_16 = sb("n1_16", [P, T, 2, C], F16)
        n2_32 = sb("n2_32", [P, T, C], F32)
        n2_16 = sb("n2_16", [P, T, 2, C], F16)
        n1T = sb("n1T", [P, 2, KT, GT], F16)
        n2T = sb("n2T", [P, 2, KT, GT], F16)
        rope_c = sb("rope_c", [P, 2, GT], F32)
        rope_s = sb("rope_s", [P, 2, GT], F32)
        qk_32 = sb("qk_32", [P, 2, GT], F32)
        q_16 = sb("q_16", [P, KT, 2, GT], F16)
        k_16 = sb("k_16", [P, KT, 2, GB, 2, N], F16)
        q_stack = sb("q_stack", [P, J, GT], F16)
        k_stack = sb("k_stack", [P, J, GB, 2, N], F16)
        v_16 = sb("v_16", [P, BP, 2, 2, J, D1], F16)
        v_diag = sb("v_diag", [P, GB, 2, 2, J, D1], F16)
        smax = sb("smax", [P, BP, H], F32)
        smaxT = sb("smaxT", [H, GT], F16)
        p_32 = sb("p_32", [P, 2, J * N], F32)
        p_16 = sb("p_16", [P, 4, 2, J * N], F16)
        rsum = sb("rsum", [P, BP, H], F32)
        o_32 = sb("o_32", [P, 2, C], F32)
        o_16 = sb("o_16", [P, BP, 2, C], F16)
        oT = sb("oT", [P, 2, KT, GT], F16)
        gated = sb("gated", [P, 2, C], F32)
        h_32 = sb("h_32", [P, 3, GT], F32)
        h_16 = sb("h_16", [P, FU, 2, GT], F16)

        ps_proj = [psum(f"ps_proj{n}", [P, GT], F32) for n in range(2)]
        ps_tok = [psum(f"ps_tok{n}", [P, 512], F32)[:, 0:C] for n in range(2)]
        ps_score = [psum(f"ps_score{n}", [P, 512], F32) for n in range(2)]
        ps_turn = [ps[:, 0:C].bitcast(F16).rearrange("p (h k n) -> p h k n", h=2, k=KT) for ps in ps_score]
        ps_pv = [psum(f"ps_pv{n}", [P, 512], F32) for n in range(2)]
        pv_out = [ps[:, 0:J * 2 * D1].rearrange("p (h e) -> p h e", e=D1) for ps in ps_pv]
        ps_smaxT = [ps[0:H, 384:384 + P] for ps in ps_pv]

        stage_h = h_16[:].rearrange("p u a n -> p (u a n)").bitcast(F32)
        stage_w1 = stage_h[:, 0:KT * F].rearrange("p (k n) -> p k n", k=KT)
        stage_w2 = stage_h[:, KT * F:KT * F + FU * C].rearrange("p (u n) -> p u n", u=FU)
        stage_q = q_stack[:].rearrange("p j n -> p (j n)").bitcast(F32)
        stage_qkvo = stage_q.rearrange("p (w k n) -> p w k n", w=4, k=KT)
        stage_k = k_stack[:].rearrange("p j b a n -> p (j b a n)").bitcast(F32)
        stage_ada = stage_k[:, 0:KT * 6 * C].rearrange("p (k n) -> p k n", k=KT)
        stage_norm = stage_k[:, KT * 6 * C:KT * 6 * C + 4 * C].rearrange("p (s n) -> p s n", s=4)
        stage_mod = oT[:].rearrange("p h k n -> p (h k n)").bitcast(F32)
        stage_mod2 = n1T[:].rearrange("p h k n -> p (h k n)").bitcast(F32)
        stage_mod = stage_mod.rearrange("p (s n) -> p s n", n=C)
        stage_mod2 = stage_mod2.rearrange("p (s n) -> p s n", n=C)[:, 0:2]

        def mod_row(s):
            return stage_mod[:, s] if s < 4 else stage_mod2[:, s - 4]

        mod_out = p_16[:].rearrange("p a h n -> p (a h n)").bitcast(F32)[:, 0:6 * C]
        mod_out = mod_out.rearrange("p (s n) -> p s n", s=6)
        cond_sb = n1_32[:, 0, :]
        cond_e = n1_32[:, 1, :]
        cond_r = n1_32[:, 2, :]
        cond_s = n1_32[:, 3, :]
        condT = n2_32[:, 0, :].rearrange("p (k b) -> p k b", k=KT)
        ada_b_sb = h_32[:].rearrange("p a n -> p (a n)")[:, 0:6 * C].rearrange("p (s n) -> p s n", s=6)

        cond_in = sem("cond_in")
        ada_in = sem("ada_in")
        wqkvo_in = sem("wqkvo_in")
        wmlp_in = sem("wmlp_in")
        rope_in = sem("rope_in")
        zeroed = sem("zeroed")
        ident_done = sem("ident_done")
        cond_exp = sem("cond_exp")
        cond_step = sem("cond_step")
        condT_ps = sem("condT_ps")
        condT_done = sem("condT_done")
        mod_ps = sem("mod_ps")
        mod_step = sem("mod_step")
        mod_stored = sem("mod_stored")
        w_hi = sem("w_hi")
        w_lo = sem("w_lo")
        w_rot = sem("w_rot")
        stacks_clear = sem("stacks_clear")
        selector = sem("selector")

        x_loaded = sem("x_loaded")
        x_res_loaded = sem("x_res_loaded")
        x_late_copied = sem("x_late_copied")
        mod1_loaded = sem("mod1_loaded")
        mod2_loaded = sem("mod2_loaded")
        mod3_loaded = sem("mod3_loaded")
        ln1_stats = sem("ln1_stats")
        ln1_var = sem("ln1_var")
        ln1_rstd = sem("ln1_rstd")
        ln1_factor = sem("ln1_factor")
        ln1_done = sem("ln1_done")
        ln1_hi = sem("ln1_hi")
        ln1_lo = sem("ln1_lo")
        ln2_stats = sem("ln2_stats")
        ln2_var = sem("ln2_var")
        ln2_rstd = sem("ln2_rstd")
        ln2_factor = sem("ln2_factor")
        ln2_done = sem("ln2_done")
        ln2_hi = sem("ln2_hi")
        ln2_lo = sem("ln2_lo")
        n1_turned = sem("n1_turned")
        n2_turned = sem("n2_turned")
        o_turned = sem("o_turned")
        n1_out = sem("n1_out")
        n2_out = sem("n2_out")
        o_part = sem("o_part")
        o_out = sem("o_out")
        qk_ps = sem("qk_ps")
        rope_half = sem("rope_half")
        rope_sum = sem("rope_sum")
        qk_hi = sem("qk_hi")
        qk_lo = sem("qk_lo")
        v_ps = sem("v_ps")
        v_hi = sem("v_hi")
        v_lo = sem("v_lo")
        hi_stacked = sem("hi_stacked")
        lo_stacked = sem("lo_stacked")
        hi_doubled = sem("hi_doubled")
        v_stacked = sem("v_stacked")
        s_ps = sem("s_ps")
        smax_done = sem("smax_done")
        smaxT_ps = sem("smaxT_ps")
        smaxT_done = sem("smaxT_done")
        smax_stacked = [sem(f"smax_stacked{n}") for n in range(2)]
        st_ps = sem("st_ps")
        exp_done = sem("exp_done")
        p_hi = sem("p_hi")
        p_lo = sem("p_lo")
        pv_ps = sem("pv_ps")
        rsum_done = sem("rsum_done")
        o_done = sem("o_done")
        o_hi = sem("o_hi")
        o_lo = sem("o_lo")
        attn_ps = sem("attn_ps")
        gated1 = sem("gated1")
        mid_done = sem("mid_done")
        h_ps = sem("h_ps")
        gelu_done = sem("gelu_done")
        h_hi = sem("h_hi")
        h_lo = sem("h_lo")
        mlp_ps = sem("mlp_ps")
        gated2 = sem("gated2")
        out_done = sem("out_done")
        stored = sem("stored")

        block = ctx.enter_context(nc.Block())

        def is_first(g):
            return isinstance(g, int) and g == 0

        def tok_v(q):
            return ps_tok[q % 2]

        def tok_wo(t):
            return ps_tok[(t + 1) % 2]

        def tok_mlp(t):
            return ps_tok[t % 2]

        def gated_wo(t):
            return gated[:, (t + 1) % 2]

        def gated_mlp(t):
            return gated[:, t % 2]

        STACK_COUNT = 16 * 2 * J

        @block.sync
        def _(sp):
            sp.dma_start(cond_sb, cond).then_inc(cond_in, 16)
            sp.dma_start(stage_ada, ada_w.rearrange("(k p) n -> p k n", p=P)).then_inc(ada_in, 16)
            sp.dma_start(ada_b_sb.rearrange("p s n -> p (s n)"), ada_b.partition_broadcast(P)).then_inc(ada_in, 16)
            for n, v in enumerate((g1, b1, g2, b2)):
                sp.dma_start(stage_norm[:, n, :], v.partition_broadcast(P)).then_inc(ada_in, 16)
            for n, w in enumerate((wq, wk, wv, wo)):
                sp.dma_start(stage_qkvo[:, n], w.rearrange("(k p) n -> p k n", p=P)).then_inc(wqkvo_in, 16)
            sp.dma_start(table[:], rope).then_inc(rope_in, 16)
            sp.dma_start(x_in[:].rearrange("p t c -> p (t c)"), x_g[0]).then_inc(x_loaded, 16)
            sp.dma_start(stage_w1, w1.rearrange("(k p) n -> p k n", p=P)).then_inc(wmlp_in, 16)
            sp.dma_start(stage_w2, w2.rearrange("(u p) n -> p u n", p=P)).then_inc(wmlp_in, 16)
            sp.wait_ge(mod_step, 15)
            sp.dma_start(mod_dram, mod_out).then_inc(mod_stored, 16)
            sp.wait_ge(mod_stored, 16)

            def load_mod(dst, g, s0, s1, done):
                sp.wait_ge(mod_stored, 16)
                src = mod_g[g][:, s0:s1, :].rearrange("b s c -> b (s c)")
                rows = src.unsqueeze(1).to_broadcast([GB, I, (s1 - s0) * C])
                sp.dma_start(dst.rearrange("p s c -> p (s c)"), rows).then_inc(done, 16)

            def restack(i):
                for part, done, ready in ((0, hi_stacked, qk_hi), (1, lo_stacked, qk_lo)):
                    for qk, src, stack, block_of in ((0, q_16, q_stack, (0, 2)), (1, k_16, k_stack, (0, 1))):
                        for kt in range(KT):
                            sp.wait_ge(ready, i * 8 + 4 * qk + 2 * kt + 2)
                            if part == qk == kt == 0 and not is_first(i):
                                sp.wait_ge(st_ps, i * GB)
                            row = 32 * block_of[part]
                            for j in range(JK):
                                sp.dma_start(stack[row:row + 32, JK * kt + j],
                                             src[32 * j:32 * j + 32, kt, part]).then_inc(done, 16)

            def restack_v(i):
                sp.wait_ge(v_hi, i * BP + BP)
                sp.wait_ge(v_lo, i * BP + BP)
                for a in range(2):
                    for b in range(2):
                        src = v_16[N * b:N * b + N, :, a].rearrange("m q h j e -> m q (h j e)")
                        dst = v_diag[N * a:N * a + N, b:GB:2, a].rearrange("m q h j e -> m q (h j e)")
                        sp.dma_start(dst, src).then_inc(v_stacked, 16)

            def stack_max(i, half):
                sp.wait_ge(smaxT_done, i * BP + 2 * half + 2)
                cols = slice(half * 2 * P, half * 2 * P + 2 * P)
                for a in range(2):
                    src = smaxT[a:H:2, cols]
                    sp.dma_start(q_stack[96 + a:97 + a, :, cols], src).then_inc(smax_stacked[half], 16)

            def iteration(i, project, attend, mlp2, norm_next):
                if attend:
                    if not is_first(i - 1):
                        sp.wait_ge(mid_done, (i - 1) * T)
                        sp.wait_ge(ln2_done, (i - 1) * T)
                        sp.wait_ge(mod_stored, 16)
                    sp.dma_start(x_res[:].rearrange("p t c -> p (t c)"), x_g[i - 1]).then_inc(x_res_loaded, 16)
                    load_mod(mod2[:], i - 1, 2, 5, mod2_loaded)
                if mlp2:
                    if not is_first(i - 2):
                        sp.wait_ge(gated2, (i - 2) * T)
                    load_mod(mod3[:], i - 2, 5, 6, mod3_loaded)
                if norm_next:
                    sp.wait_ge(ln1_done, i * T + T)
                    sp.wait_ge(mod_stored, 16)
                    sp.dma_start(x_in[:].rearrange("p t c -> p (t c)"), x_g[i + 1]).then_inc(x_loaded, 16)
                    load_mod(mod1[:], i + 1, 0, 2, mod1_loaded)
                if attend:
                    stack_max(i - 1, 0)
                    stack_max(i - 1, 1)
                if project:
                    restack(i)
                    if not is_first(i):
                        sp.wait_ge(pv_ps, i * BP)
                    restack_v(i)
                if mlp2:
                    sp.wait_ge(out_done, (i - 1) * T)
                    sp.wait_ge(mod_stored, 16)
                    sp.dma_start(out_g[i - 2], out_sb[:].rearrange("p t c -> p (t c)")).then_inc(stored, 16)
                if attend:
                    sp.wait_ge(mid_done, i * T)
                    sp.dma_start(x_late[:], x_mid[:]).then_inc(x_late_copied, 16)

            load_mod(mod1[:], 0, 0, 2, mod1_loaded)
            sp.wait_ge(selector, 1)
            sp.wait_ge(stacks_clear, 3)
            iteration(0, True, False, False, True)
            iteration(1, True, True, False, True)
            iteration(2, True, True, True, True)
            with sp.Fori(3, G - 1) as i:
                iteration(i, True, True, True, True)
            iteration(G - 1, True, True, True, False)
            iteration(G, False, True, True, False)
            iteration(G + 1, False, False, True, False)
            sp.wait_ge(stored, 16 * G)

        @block.gpsimd
        def _(pool):
            pool.memset(minus_half[:], -0.5).then_inc(zeroed, 1)
            pool.memset(ident16[:], 0.0).then_inc(zeroed, 1)
            pool.memset(ident32[:], 0.0).then_inc(zeroed, 1)
            pool.wait_ge(zeroed, 3)
            for m in (ident16, ident32):
                pool.affine_select(out=m[:], in_=m[:], compare_op=ALU.not_equal, fill=1.0, base=0,
                                   pattern=[[-1, P]], channel_multiplier=1).then_inc(ident_done, 1)
            pool.memset(v_16[:, :, :, 0, :, D:D1].rearrange("p q a j e -> p (q a) (j e)"), 1.0).then_inc(stacks_clear, 1)
            pool.memset(v_16[:, :, :, 1, :, D:D1].rearrange("p q a j e -> p (q a) (j e)"), 0.0).then_inc(stacks_clear, 1)
            pool.memset(v_diag[:].rearrange("p b a h j e -> p (b a h j e)"), 0.0).then_inc(stacks_clear, 1)
            pool.wait_ge(mod_ps, 3)
            pool.wait_ge(mod_step, 15)
            pool.memset(k_stack[:].rearrange("p j b a n -> p (j b a n)"), 0.0).then_inc(zeroed, 1)
            pool.wait_ge(zeroed, 4)
            k_sel = k_stack[96:98].rearrange("p j b a n -> p (j b) a n")
            pool.affine_select(out=k_sel, in_=k_sel, compare_op=ALU.not_equal, fill=-MAX_SCALE, base=0,
                               pattern=[[0, J * GB], [-1, 2], [0, N]], channel_multiplier=1).then_inc(selector, 1)

            pool.wait_ge(selector, 1)

            def norm_rstd(k, g, var, done):
                pool.wait_ge(var, g + 1)
                pool.tensor_tensor(rstd[:, k], var_eps[:, k], minus_half[:], ALU.pow).then_inc(done, 1)

            def norm_lo(g, n32, n16, hi, lo):
                for t in range(T):
                    pool.wait_ge(hi, g * T + t + 1)
                    pool.tensor_tensor(n16[:, t, 1], n32[:, t], n16[:, t, 0], ALU.subtract).then_inc(lo, 1)

            def rotary_sum(i, c):
                pool.wait_ge(rope_half, i * 8 + 2 * c + 2)
                if c >= 2 or not is_first(i):
                    pool.wait_ge(qk_lo, i * 8 + 2 * c - 2)
                pool.tensor_tensor(qk_32[:, c % 2], rope_c[:, c % 2], rope_s[:, c % 2], ALU.add).then_inc(rope_sum, 1)

            def q_low(i, c):
                pool.wait_ge(qk_hi, i * 8 + 2 * c + 2)
                if c == 0 and not is_first(i):
                    pool.wait_ge(lo_stacked, i * STACK_COUNT)
                pool.tensor_tensor(q_16[:, c, 1], qk_32[:, c % 2], q_16[:, c, 0], ALU.subtract).then_inc(qk_lo, 2)

            def o_low(g, q):
                pool.wait_ge(o_hi, g * BP + q + 1)
                pool.tensor_tensor(o_16[:, q, 1], o_32[:, q % 2], o_16[:, q, 0], ALU.subtract).then_inc(o_lo, 1)

            def residual_2(g, t):
                pool.wait_ge(gated2, g * T + t + 1)
                if t == 0:
                    pool.wait_ge(x_late_copied, g * 16 + 16)
                    if not is_first(g):
                        pool.wait_ge(stored, g * 16)
                pool.tensor_tensor(out_sb[:, t], gated_mlp(t), x_late[:, t], ALU.add).then_inc(out_done, 1)

            def iteration(i, project, attend, mlp2, norm_next):
                if project:
                    rotary_sum(i, 0)
                    q_low(i, 0)
                    rotary_sum(i, 1)
                    q_low(i, 1)
                    rotary_sum(i, 2)
                if attend:
                    o_low(i - 1, 0)
                if project:
                    rotary_sum(i, 3)
                if attend:
                    for q in range(1, BP):
                        o_low(i - 1, q)
                if mlp2:
                    residual_2(i - 2, 0)
                if attend:
                    for t in range(T):
                        pool.wait_ge(gated1, (i - 1) * T + t + 1)
                        if t == 0:
                            pool.wait_ge(x_res_loaded, i * 16)
                            if not is_first(i - 1):
                                pool.wait_ge(x_late_copied, (i - 1) * 16)
                        pool.tensor_tensor(x_mid[:, t], gated_wo(t), x_res[:, t], ALU.add).then_inc(mid_done, 1)
                    norm_rstd(1, i - 1, ln2_var, ln2_rstd)
                    if mlp2:
                        residual_2(i - 2, 1)
                    norm_lo(i - 1, n2_32, n2_16, ln2_hi, ln2_lo)
                elif mlp2:
                    residual_2(i - 2, 1)
                if mlp2:
                    residual_2(i - 2, 2)
                    residual_2(i - 2, 3)
                if norm_next:
                    norm_rstd(0, i + 1, ln1_var, ln1_rstd)
                    norm_lo(i + 1, n1_32, n1_16, ln1_hi, ln1_lo)

            norm_rstd(0, 0, ln1_var, ln1_rstd)
            norm_lo(0, n1_32, n1_16, ln1_hi, ln1_lo)
            iteration(0, True, False, False, True)
            iteration(1, True, True, False, True)
            iteration(2, True, True, True, True)
            with pool.Fori(3, G - 1) as i:
                iteration(i, True, True, True, True)
            iteration(G - 1, True, True, True, False)
            iteration(G, False, True, True, False)
            iteration(G + 1, False, False, True, False)

        @block.scalar
        def _(act):
            act.wait_ge(cond_in, 16)
            act.activation(cond_e, cond_sb, ACT.Exp, scale=-1.0).then_inc(cond_exp, 1)
            act.wait_ge(condT_ps, 1)
            act.activation(condT, ps_score[0][:, 0:C].rearrange("p (k b) -> p k b", k=KT), ACT.Copy).then_inc(condT_done, 1)
            act.wait_ge(wqkvo_in, 64)
            for n in range(2):
                act.activation(w_qk[:, 0, 2 * n], stage_qkvo[:, n], ACT.Copy, scale=W_SCALE).then_inc(w_hi, 1)
            for kt in range(KT):
                act.activation(w_v[:, 0, kt].rearrange("p (a j r) -> p a j r", a=2, r=D),
                               stage_qkvo[:, 2, kt].rearrange("p (j a r) -> p a j r", a=2, r=D),
                               ACT.Copy, scale=V_SCALE).then_inc(w_hi, 1)
            act.activation(w_o[:, 0], stage_qkvo[:, 3], ACT.Copy, scale=W_SCALE).then_inc(w_hi, 1)
            act.wait_ge(wmlp_in, 32)
            act.activation(w_1[:, 0], stage_w1, ACT.Copy, scale=W_SCALE).then_inc(w_hi, 1)
            act.activation(w_2[:, 0], stage_w2, ACT.Copy, scale=W_SCALE).then_inc(w_hi, 1)

            def norm_hi(g, n32, n16, done, hi):
                for t in range(T):
                    act.wait_ge(done, g * T + t + 1)
                    act.activation(n16[:, t, 0], n32[:, t], ACT.Copy).then_inc(hi, 1)

            def q_k_high(i, c):
                act.wait_ge(rope_sum, i * 4 + c + 1)
                if c == 0 and not is_first(i):
                    act.wait_ge(hi_stacked, i * STACK_COUNT)
                    act.wait_ge(lo_stacked, i * STACK_COUNT)
                if c < 2:
                    act.activation(q_16[:, c, 0], qk_32[:, c % 2], ACT.Copy).then_inc(qk_hi, 2)
                else:
                    for a in range(2):
                        act.activation(k_16[:, c - 2, 0, :, a], qk_32[:, c % 2].rearrange("p (b n) -> p b n", n=N),
                                       ACT.Identity, scale=parity[:, a:a + 1]).then_inc(qk_hi, 1)

            def v_high(i, q):
                act.wait_ge(v_ps, i * BP + q + 1)
                if q == 0 and not is_first(i):
                    act.wait_ge(v_stacked, i * 64)
                act.activation(v_16[:, q, :, 0, :, 0:D], tok_v(q).rearrange("p (a j r) -> p a j r", a=2, r=D),
                               ACT.Copy).then_inc(v_hi, 1)

            def max_out(g, q):
                act.wait_ge(smaxT_ps, g * BP + q + 1)
                if q == 0 and not is_first(g):
                    for half in range(2):
                        act.wait_ge(smax_stacked[half], g * 32)
                act.activation(smaxT[:, q * P:q * P + P], ps_smaxT[q % 2], ACT.Copy,
                               scale=1.0 / MAX_SCALE).then_inc(smaxT_done, 1)

            def softmax(g, b):
                act.wait_ge(st_ps, g * GB + b + 1)
                if b >= 2 or not is_first(g):
                    act.wait_ge(p_lo, g * GB + b - 1)
                act.activation(p_32[:, b % 2], ps_score[b % 2][:], ACT.Exp, scale=EXP_SCALE).then_inc(exp_done, 1)
                act.wait_ge(exp_done, g * GB + b + 1)
                if b % 2 == 0 and (b >= 4 or not is_first(g)):
                    act.wait_ge(pv_ps, g * BP + b // 2 - 1)
                act.activation(p_16[:, b % 4, 0], p_32[:, b % 2], ACT.Copy).then_inc(p_hi, 1)

            def o_high(g, q):
                act.wait_ge(o_done, g * BP + q + 1)
                act.activation(o_16[:, q, 0], o_32[:, q % 2], ACT.Copy).then_inc(o_hi, 1)

            def iteration(i, project, attend, mlp2, norm_next):
                g = i - 1
                if project:
                    for t in range(T):
                        act.wait_ge(n1_turned, i * T + t + 1)
                        dst = n1T[:].rearrange("p h k (b t i) -> p (h k) b t i", t=T, i=I)[:, :, :, t]
                        act.activation(dst, ps_turn[t % 2].rearrange("p h k (b i) -> p (h k) b i", i=I),
                                       ACT.Copy).then_inc(n1_out, 1)
                    q_k_high(i, 0)
                if attend:
                    max_out(g, 0)
                    max_out(g, 1)
                if project:
                    q_k_high(i, 1)
                if attend:
                    max_out(g, 2)
                    max_out(g, 3)
                    softmax(g, 0)
                    softmax(g, 1)
                if project:
                    q_k_high(i, 2)
                if attend:
                    softmax(g, 2)
                    softmax(g, 3)
                    o_high(g, 0)
                    softmax(g, 4)
                    softmax(g, 5)
                if project:
                    q_k_high(i, 3)
                if attend:
                    o_high(g, 1)
                if project:
                    v_high(i, 0)
                    v_high(i, 1)
                if attend:
                    softmax(g, 6)
                    softmax(g, 7)
                    o_high(g, 2)
                if project:
                    v_high(i, 2)
                    v_high(i, 3)
                if attend:
                    o_high(g, 3)
                    for q in range(BP):
                        act.wait_ge(o_turned, g * BP + q + 1)
                        for b in range(2):
                            src = ps_turn[q % 2].rearrange("p h k (b t i) -> p (h k) b t i", b=2, i=I)[:, :, b]
                            dst = oT[:].rearrange("p h k (t b i) -> p (h k) b t i", t=T, i=I)[:, :, 2 * q + b]
                            act.activation(dst, src, ACT.Copy).then_inc(o_part if b == 0 else o_out, 1)
                    norm_hi(g, n2_32, n2_16, ln2_done, ln2_hi)
                    for t in range(T):
                        act.wait_ge(n2_turned, g * T + t + 1)
                        act.activation(n2T[:, :, :, t * P:t * P + P].rearrange("p h k n -> p (h k) n"),
                                       ps_turn[t % 2].rearrange("p h k n -> p (h k) n"), ACT.Copy).then_inc(n2_out, 1)
                    for u in range(FU):
                        act.wait_ge(h_ps, g * FU + u + 1)
                        if u >= 2 or not is_first(g):
                            act.wait_ge(h_lo, g * FU + u - 1)
                        act.activation(h_32[:, u % 2], ps_proj[u % 2][:], ACT.Gelu, scale=GELU_SCALE).then_inc(gelu_done, 1)
                        act.wait_ge(gelu_done, g * FU + u + 1)
                        if u == 0 and not is_first(g):
                            act.wait_ge(mlp_ps, g * T)
                        act.activation(h_16[:, u, 0], h_32[:, u % 2], ACT.Copy).then_inc(h_hi, 1)
                        if u == 3 and norm_next:
                            norm_hi(i + 1, n1_32, n1_16, ln1_done, ln1_hi)
                elif norm_next:
                    norm_hi(i + 1, n1_32, n1_16, ln1_done, ln1_hi)

            norm_hi(0, n1_32, n1_16, ln1_done, ln1_hi)
            iteration(0, True, False, False, True)
            iteration(1, True, True, False, True)
            iteration(2, True, True, True, True)
            with act.Fori(3, G - 1) as i:
                iteration(i, True, True, True, True)
            iteration(G - 1, True, True, True, False)
            iteration(G, False, True, True, False)
            iteration(G + 1, False, False, True, False)

        @block.vector
        def _(dve):
            dve.wait_ge(cond_exp, 1)
            dve.tensor_scalar(cond_e, cond_e, 1.0, None, ALU.add).then_inc(cond_step, 1)
            dve.wait_ge(cond_step, 1)
            dve.reciprocal(cond_r, cond_e).then_inc(cond_step, 1)
            dve.wait_ge(cond_step, 2)
            dve.tensor_tensor(cond_s, cond_sb, cond_r, ALU.mult).then_inc(cond_step, 1)

            def norm_stats(k, g, src, in_done, in_count, stats_done, var_done):
                for t in range(T):
                    if not (isinstance(in_count[t], int) and in_count[t] == 0):
                        dve.wait_ge(in_done, in_count[t])
                    dve.bn_stats(stats[:, k, t], src[:, t]).then_inc(stats_done, 1)
                dve.wait_ge(stats_done, g * (2 * T + 1) + T)
                dve.memset(var_eps[:, k], EPS).then_inc(stats_done, 1)
                for t in range(T):
                    dve.bn_aggr(moments[:, k, t], stats[:, k, t]).then_inc(stats_done, 1)
                dve.wait_ge(stats_done, g * (2 * T + 1) + 2 * T + 1)
                dve.tensor_tensor(var_eps[:, k], moments[:, k, :, 1], var_eps[:, k], ALU.add).then_inc(var_done, 1)

            def norm_apply(k, g, src, mod, m0, n32, factor, rstd_done, done):
                for t in range(T):
                    dve.scalar_tensor_tensor(n32[:, t], src[:, t], moments[:, k, t, 0:1], mod[:, m0],
                                             ALU.subtract, ALU.mult).then_inc(factor, 1)
                dve.wait_ge(rstd_done, g + 1)
                for t in range(T):
                    dve.wait_ge(factor, g * T + t + 1)
                    dve.scalar_tensor_tensor(n32[:, t], n32[:, t], rstd[:, k, t:t + 1], mod[:, m0 + 1],
                                             ALU.mult, ALU.add).then_inc(done, 1)

            def norm1(g):
                norm_stats(0, g, x_in, x_loaded, [g * 16 + 16, 0, 0, 0], ln1_stats, ln1_var)
                dve.wait_ge(mod1_loaded, g * 16 + 16)
                if not is_first(g):
                    dve.wait_ge(ln1_lo, g * T)
                norm_apply(0, g, x_in, mod1, 0, n1_32, ln1_factor, ln1_rstd, ln1_done)

            dve.wait_ge(ada_in, 16 * 6)
            for n, ps in enumerate((ps_proj[0], ps_proj[1], ps_score[1])):
                dve.wait_ge(mod_ps, n + 1)
                dve.tensor_tensor(stage_mod[:, 2 * n:2 * n + 2] if n < 2 else stage_mod2, ps[:].rearrange("p (s c) -> p s c", s=2),
                                  ada_b_sb[:, 2 * n:2 * n + 2], ALU.add).then_inc(mod_step, 1)
            dve.wait_ge(mod_step, 3)
            for n, (fac, sh) in enumerate(((0, 1), (3, 4))):
                scale, shift = mod_row(3 * n + 1), mod_row(3 * n)
                dve.scalar_tensor_tensor(mod_out[:, fac], scale, 1.0, stage_norm[:, 2 * n], ALU.add, ALU.mult).then_inc(mod_step, 1)
                dve.scalar_tensor_tensor(mod_out[:, sh], scale, 1.0, stage_norm[:, 2 * n + 1], ALU.add, ALU.mult).then_inc(mod_step, 1)
                dve.wait_ge(mod_step, 3 + 5 * n + 2)
                dve.tensor_tensor(mod_out[:, sh], mod_out[:, sh], shift, ALU.add).then_inc(mod_step, 1)
                dve.wait_ge(mod_step, 3 + 5 * n + 3)
                for m in (fac, sh):
                    dve.tensor_scalar(mod_out[:, m], mod_out[:, m], X_SCALE, None, ALU.mult).then_inc(mod_step, 1)
            dve.tensor_scalar(mod_out[:, 2], mod_row(2), GATE1_SCALE, None, ALU.mult).then_inc(mod_step, 1)
            dve.tensor_scalar(mod_out[:, 5], mod_row(5), GATE2_SCALE, None, ALU.mult).then_inc(mod_step, 1)

            def low(dst, src, hi, scale, count):
                dve.wait_ge(w_hi, count)
                dve.scalar_tensor_tensor(dst, src, scale, hi, ALU.mult, ALU.subtract).then_inc(w_lo, 1)

            count = 0
            for n in range(2):
                count += 1
                low(w_qk[:, 1, 2 * n], stage_qkvo[:, n], w_qk[:, 0, 2 * n], W_SCALE, count)
            for kt in range(KT):
                count += 1
                for a in range(2):
                    low(w_v[:, 1, kt].rearrange("p (a j r) -> p a j r", a=2, r=D)[:, a],
                        stage_qkvo[:, 2, kt].rearrange("p (j a r) -> p a j r", a=2, r=D)[:, a],
                        w_v[:, 0, kt].rearrange("p (a j r) -> p a j r", a=2, r=D)[:, a], V_SCALE, count)
            for dst, src in ((w_o, stage_qkvo[:, 3]), (w_1, stage_w1), (w_2, stage_w2)):
                count += 1
                low(dst[:, 1], src, dst[:, 0], W_SCALE, count)
                if dst is w_o:
                    dve.wait_ge(w_lo, 7)
                    for n in range(2):
                        for part in range(2):
                            plain = w_qk[:, part, 2 * n].rearrange("p k (h r) -> p (k h) r", r=D)
                            turnd = w_qk[:, part, 2 * n + 1].rearrange("p k (h r) -> p (k h) r", r=D)
                            dve.tensor_copy(turnd[:, :, 0:D // 2], plain[:, :, 1:D:2]).then_inc(w_rot, 1)
                            dve.tensor_copy(turnd[:, :, D // 2:D], plain[:, :, 0:D:2]).then_inc(w_rot, 1)
                    norm1(0)
            dve.wait_ge(rope_in, 16)

            def rotary(i, u):
                c = u // 2
                dve.wait_ge(qk_ps, i * 8 + u + 1)
                if c >= 2 or not is_first(i):
                    dve.wait_ge(rope_sum, i * 4 + c - 1)
                dst = (rope_c if u % 2 == 0 else rope_s)[:, c % 2].rearrange("p (b n) -> p b n", b=GB)
                dve.tensor_tensor(dst, ps_proj[u % 2][:].rearrange("p (b n) -> p b n", b=GB),
                                  rope_sb[:, u % 2].unsqueeze(1).to_broadcast([P, GB, N]), ALU.mult).then_inc(rope_half, 1)

            def k_low(i, c):
                dve.wait_ge(qk_hi, i * 8 + 2 * c + 2)
                for a in range(2):
                    dve.scalar_tensor_tensor(k_16[:, c - 2, 1, :, a], qk_32[:, c % 2].rearrange("p (b n) -> p b n", n=N),
                                             parity[:, a:a + 1], k_16[:, c - 2, 0, :, a], ALU.mult,
                                             ALU.subtract).then_inc(qk_lo, 1)

            def v_low(i, q):
                dve.wait_ge(v_hi, i * BP + q + 1)
                dve.tensor_tensor(v_16[:, q, :, 1, :, 0:D], tok_v(q).rearrange("p (a j r) -> p a j r", a=2, r=D),
                                  v_16[:, q, :, 0, :, 0:D], ALU.subtract).then_inc(v_lo, 1)

            def h_low(g, u):
                dve.wait_ge(h_hi, g * FU + u + 1)
                dve.tensor_tensor(h_16[:, u, 1], h_32[:, u % 2], h_16[:, u, 0], ALU.subtract).then_inc(h_lo, 1)

            def score_max(g, s):
                dve.wait_ge(s_ps, g * 8 + s + 1)
                dve.tensor_reduce(smax[:, s // 2, J * (s % 2):J * (s % 2) + J],
                                  ps_score[s % 2][:].rearrange("p (h m) -> p h m", m=N), AX_X, ALU.max).then_inc(smax_done, 1)

            def p_low(g, b):
                dve.wait_ge(p_hi, g * GB + b + 1)
                dve.tensor_tensor(p_16[:, b % 4, 1], p_32[:, b % 2], p_16[:, b % 4, 0], ALU.subtract).then_inc(p_lo, 1)

            def attn_out(g, q):
                pv = pv_out[q % 2]
                dve.wait_ge(pv_ps, g * BP + q + 1)
                dve.reciprocal(rsum[:, q], pv[:, :, D]).then_inc(rsum_done, 1)
                dve.wait_ge(rsum_done, g * BP + q + 1)
                if q >= 2 or not is_first(g):
                    dve.wait_ge(o_lo, g * BP + q - 1)
                dve.tensor_tensor(o_32[:, q % 2].rearrange("p (h r) -> p h r", r=D), pv[:, :, 0:D],
                                  rsum[:, q].unsqueeze(2).to_broadcast([P, H, D]), ALU.mult).then_inc(o_done, 1)

            def gate_1(g, t, mlp2):
                dve.wait_ge(attn_ps, g * T + t + 1)
                if t == 0:
                    dve.wait_ge(mod2_loaded, g * 16 + 16)
                if t == 0 and mlp2 and not is_first(g - 1):
                    dve.wait_ge(out_done, (g - 1) * T)
                elif t == 1 and mlp2:
                    dve.wait_ge(out_done, (g - 1) * T + 1)
                elif t >= 2:
                    dve.wait_ge(mid_done, g * T + t - 1)
                dve.tensor_tensor(gated_wo(t), tok_wo(t), mod2[:, 0], ALU.mult).then_inc(gated1, 1)

            def gate_2(g, t, attend):
                dve.wait_ge(mlp_ps, g * T + t + 1)
                if t == 0:
                    dve.wait_ge(mod3_loaded, g * 16 + 16)
                if t == 0 and not is_first(g):
                    dve.wait_ge(out_done, g * T)
                if t == 0:
                    dve.wait_ge(mid_done, (g + 1) * T)
                elif t in (1, 2) and attend:
                    dve.wait_ge(mid_done, (g + 1) * T + t + 2)
                elif t >= 2:
                    dve.wait_ge(out_done, g * T + t - 1)
                dve.tensor_tensor(gated_mlp(t), tok_mlp(t), mod3[:, 0], ALU.mult).then_inc(gated2, 1)

            def double_high(i, stack, row, first):
                if first:
                    dve.wait_ge(hi_stacked, (i + 1) * STACK_COUNT)
                view = stack[:].rearrange("p j n -> p (j n)") if stack is q_stack else \
                    stack[:].rearrange("p j b a n -> p (j b a n)")
                dve.tensor_copy(view[row:row + 32], view[0:32]).then_inc(hi_doubled, 1)

            def iteration(i, project, attend, mlp2, norm_next):
                g = i - 1
                for n in range(4):
                    if attend:
                        score_max(g, 2 * n)
                        score_max(g, 2 * n + 1)
                    if project:
                        rotary(i, n)
                if project:
                    rotary(i, 4)
                    rotary(i, 5)
                if attend:
                    p_low(g, 0)
                    p_low(g, 1)
                if project:
                    rotary(i, 6)
                    k_low(i, 2)
                if attend:
                    p_low(g, 2)
                    p_low(g, 3)
                    attn_out(g, 0)
                if project:
                    rotary(i, 7)
                if attend:
                    p_low(g, 4)
                    p_low(g, 5)
                    attn_out(g, 1)
                if project:
                    k_low(i, 3)
                    v_low(i, 0)
                    v_low(i, 1)
                if attend:
                    p_low(g, 6)
                    p_low(g, 7)
                    attn_out(g, 2)
                if project:
                    v_low(i, 2)
                    v_low(i, 3)
                if attend:
                    attn_out(g, 3)
                if mlp2:
                    gate_2(i - 2, 0, attend)
                if attend:
                    for t in range(T):
                        gate_1(g, t, mlp2)
                    norm_stats(1, g, x_mid, mid_done, [g * T + t + 1 for t in range(T)], ln2_stats, ln2_var)
                if mlp2:
                    gate_2(i - 2, 1, attend)
                if attend:
                    if not is_first(g):
                        dve.wait_ge(ln2_lo, g * T)
                    norm_apply(1, g, x_mid, mod2, 1, n2_32, ln2_factor, ln2_rstd, ln2_done)
                if mlp2:
                    gate_2(i - 2, 2, attend)
                    gate_2(i - 2, 3, attend)
                if norm_next:
                    norm1(i + 1)
                for u in range(FU):
                    if attend:
                        h_low(g, u)
                    if project and u == 4:
                        double_high(i, q_stack, 32, True)
                    if project and u == 6:
                        double_high(i, k_stack, 64, False)

            iteration(0, True, False, False, True)
            iteration(1, True, True, False, True)
            iteration(2, True, True, True, True)
            with dve.Fori(3, G - 1) as i:
                iteration(i, True, True, True, True)
            iteration(G - 1, True, True, True, False)
            iteration(G, False, True, True, False)
            iteration(G + 1, False, False, True, False)

        @block.tensor
        def _(pe):
            PARTS = ((0, 0), (0, 1), (1, 0))

            pe.wait_ge(ident_done, 2)
            pe.wait_ge(cond_step, 3)
            for kt in range(KT):
                mm = pe.transpose(ps_score[0][:, kt * P:kt * P + P], cond_s[:, kt * P:kt * P + P], ident32[:])
            mm.then_inc(condT_ps, 1)
            pe.wait_ge(condT_done, 1)
            pe.wait_ge(ada_in, 16 * 6)
            for n, ps in enumerate((ps_proj[0], ps_proj[1], ps_score[1])):
                for kt in range(KT):
                    mm = pe.matmul(ps[:], condT[:, kt], stage_ada[:, kt, n * 512:n * 512 + 512],
                                   start=(kt == 0), stop=(kt == KT - 1))
                mm.then_inc(mod_ps, 1)
            pe.wait_ge(mod_step, 3)
            pe.wait_ge(w_lo, 9)
            pe.wait_ge(w_rot, 8)

            def turn(t, src, done):
                for part in range(2):
                    for kt in range(KT):
                        mm = pe.transpose(ps_turn[t % 2][:, part, kt], src[:, part, kt * P:kt * P + P], ident16[:])
                mm.then_inc(done, 1)

            def qk_unit(i, u):
                c, rot = u // 2, u % 2
                if u >= 2:
                    pe.wait_ge(rope_half, i * 8 + u - 1)
                elif u == 0 and not is_first(i) and not is_first(i - 1):
                    pe.wait_ge(gelu_done, (i - 1) * FU)
                if u == 0:
                    pe.wait_ge(n1_out, i * T + T)
                w = w_qk[:, :, 2 * (c // 2) + rot, :, (c % 2) * P:(c % 2) * P + P]
                for n, (a, b) in enumerate(PARTS):
                    for kt in range(KT):
                        mm = pe.matmul(ps_proj[u % 2][:], w[:, a, kt], n1T[:, b, kt],
                                       start=(n == 0 and kt == 0), stop=(n == 2 and kt == KT - 1))
                mm.then_inc(qk_ps, 1)

            def v_unit(i, q, mlp2):
                if q >= 2:
                    pe.wait_ge(v_lo, i * BP + q - 1)
                elif q == 0 and not is_first(i) and not is_first(i - 1):
                    pe.wait_ge(gated1, (i - 1) * T)
                    if mlp2 and not is_first(i - 2):
                        pe.wait_ge(gated2, (i - 2) * T)
                for n, (a, b) in enumerate(PARTS):
                    for kt in range(KT):
                        mm = pe.matmul(tok_v(q), n1T[:, a, kt, q * P:q * P + P], w_v[:, b, kt],
                                       start=(n == 0 and kt == 0), stop=(n == 2 and kt == KT - 1))
                mm.then_inc(v_ps, 1)

            def mlp1_unit(g, u, project):
                if u >= 2:
                    pe.wait_ge(gelu_done, g * FU + u - 1)
                elif u == 0:
                    pe.wait_ge(n2_out, g * T + T)
                    if project:
                        pe.wait_ge(rope_half, (g + 2) * 8)
                for n, (a, b) in enumerate(PARTS):
                    for kt in range(KT):
                        mm = pe.matmul(ps_proj[u % 2][:], w_1[:, a, kt, u * P:u * P + P], n2T[:, b, kt],
                                       start=(n == 0 and kt == 0), stop=(n == 2 and kt == KT - 1))
                mm.then_inc(h_ps, 1)

            def mlp2_tile(g, t, project, attend):
                if t == 0:
                    if project:
                        pe.wait_ge(v_lo, (g + 2) * BP + 3)
                    else:
                        pe.wait_ge(gated1, (g + 1) * T)
                        pe.wait_ge(gated2, g * T)
                    pe.wait_ge(h_lo, g * FU + FU)
                elif t == 3 or not attend:
                    if t >= 2:
                        pe.wait_ge(gated2, g * T + t - 1)
                else:
                    pe.wait_ge(gated1, (g + 1) * T + t + 2)
                for u in range(FU):
                    for n, (a, b) in enumerate(PARTS):
                        mm = pe.matmul(tok_mlp(t), h_16[:, u, a, t * P:t * P + P], w_2[:, b, u],
                                       start=(u == 0 and n == 0), stop=(u == FU - 1 and n == 2))
                mm.then_inc(mlp_ps, 1)

            def score_unit(g, s, project):
                q, half = s // 2, s % 2
                if s >= 2:
                    pe.wait_ge(smax_done, g * 8 + s - 1)
                elif s == 0:
                    if project:
                        pe.wait_ge(n1_out, (g + 2) * T)
                    pe.wait_ge(lo_stacked, (g + 1) * STACK_COUNT)
                    pe.wait_ge(hi_doubled, (g + 1) * 2)
                for j in range(JK):
                    for b in range(2):
                        jj, cols = JK * half + j, slice(N * (2 * q + b), N * (2 * q + b) + N)
                        mm = pe.matmul(ps_score[s % 2][N * b:N * b + N, 2 * N * j:2 * N * j + 2 * N],
                                       q_stack[0:96, jj, cols], k_stack[0:96, jj, 2 * q + b].rearrange("p a n -> p (a n)"),
                                       start=True, stop=True)
                mm.then_inc(s_ps, 1)

            def max_turn(g, q):
                pe.wait_ge(smax_done, g * 8 + 2 * q + 2)
                if q >= 2:
                    pe.wait_ge(smaxT_done, g * BP + q - 1)
                elif q == 0 and not is_first(g):
                    pe.wait_ge(o_done, g * BP)
                pe.transpose(ps_smaxT[q % 2], smax[:, q], ident32[:]).then_inc(smaxT_ps, 1)

            def softmax_unit(g, b):
                if b >= 2:
                    pe.wait_ge(exp_done, g * GB + b - 1)
                elif b == 0:
                    pe.wait_ge(smax_done, g * 8 + 8)
                if b % 4 == 0:
                    pe.wait_ge(smax_stacked[b // 4], g * 32 + 32)
                cols = slice(N * b, N * b + N)
                for j in range(J):
                    mm = pe.matmul(ps_score[b % 2][:, N * j:N * j + N], k_stack[0:98, j, b].rearrange("p a n -> p (a n)"),
                                   q_stack[0:98, j, cols], start=True, stop=True)
                mm.then_inc(st_ps, 1)

            def pv_unit(g, q):
                pe.wait_ge(p_lo, g * GB + 2 * q + 2)
                if q >= 2:
                    pe.wait_ge(o_done, g * BP + q - 1)
                elif q == 0:
                    pe.wait_ge(v_stacked, g * 64 + 64)
                    pe.wait_ge(smaxT_done, g * BP + BP)
                for b in range(2):
                    for j in range(J):
                        for n, (a, c) in enumerate(PARTS):
                            mm = pe.matmul(pv_out[q % 2][N * b:N * b + N, 2 * j:2 * j + 2, :],
                                           p_16[:, (2 * q + b) % 4, a, N * j:N * j + N],
                                           v_diag[:, 2 * q + b, :, c, j, :], start=(n == 0), stop=(n == 2))
                mm.then_inc(pv_ps, 1)

            def wo_unit(g, t, project, mlp2):
                if t == 0:
                    pe.wait_ge(o_out, g * BP + BP)
                    if project:
                        pe.wait_ge(v_lo, (g + 2) * BP)
                elif t == 1 and mlp2:
                    pe.wait_ge(gated2, (g - 1) * T + 1)
                elif t >= 2:
                    pe.wait_ge(gated1, g * T + t - 1)
                for n, (a, b) in enumerate(PARTS):
                    for kt in range(KT):
                        mm = pe.matmul(tok_wo(t), oT[:, a, kt, t * P:t * P + P], w_o[:, b, kt],
                                       start=(n == 0 and kt == 0), stop=(n == 2 and kt == KT - 1))
                mm.then_inc(attn_ps, 1)

            def iteration(i, project, attend, mlp2, norm_next):
                g = i - 1

                def qk(u):
                    if project:
                        qk_unit(i, u)

                def vv(*qs):
                    if project:
                        for q in qs:
                            v_unit(i, q, mlp2)

                def scores(*ss):
                    if attend:
                        for s in ss:
                            score_unit(g, s, project)

                def maxima(*qs):
                    if attend:
                        for q in qs:
                            max_turn(g, q)

                def soft(*bs):
                    if attend:
                        for b in bs:
                            softmax_unit(g, b)

                def pv(q):
                    if attend:
                        pv_unit(g, q)

                if project:
                    for t in range(T):
                        if t >= 2:
                            pe.wait_ge(n1_out, i * T + t - 1)
                        pe.wait_ge(ln1_lo, i * T + t + 1)
                        turn(t, n1_16[:, t], n1_turned)
                scores(0, 1)
                qk(0)
                scores(2, 3)
                qk(1)
                scores(4, 5)
                qk(2)
                maxima(0, 1)
                scores(6, 7)
                qk(3)
                maxima(2, 3)
                qk(4)
                qk(5)
                soft(0, 1)
                qk(6)
                soft(2, 3)
                pv(0)
                qk(7)
                soft(4, 5)
                pv(1)
                vv(0, 1)
                soft(6, 7)
                pv(2)
                vv(2, 3)
                pv(3)
                if mlp2:
                    mlp2_tile(i - 2, 0, project, attend)
                if attend:
                    for q in range(BP):
                        if q >= 2:
                            pe.wait_ge(o_out, g * BP + q - 1)
                        pe.wait_ge(o_lo, g * BP + q + 1)
                        turn(q, o_16[:, q], o_turned)
                    for t in range(T):
                        wo_unit(g, t, project, mlp2)
                if mlp2:
                    for t in range(1, T):
                        mlp2_tile(i - 2, t, project, attend)
                if attend:
                    for t in range(T):
                        if t >= 2:
                            pe.wait_ge(n2_out, g * T + t - 1)
                        pe.wait_ge(ln2_lo, g * T + t + 1)
                        turn(t, n2_16[:, t], n2_turned)
                    for u in range(FU):
                        mlp1_unit(g, u, project)

            iteration(0, True, False, False, True)
            iteration(1, True, True, False, True)
            iteration(2, True, True, True, True)
            with pe.Fori(3, G - 1) as i:
                iteration(i, True, True, True, True)
            iteration(G - 1, True, True, True, False)
            iteration(G, False, True, True, False)
            iteration(G + 1, False, False, True, False)


_INS = ['x', 'cond_1024', 'L0_cond_norm1_g', 'L0_cond_norm1_b', 'L0_cond_Wq', 'L0_cond_Wk', 'L0_cond_Wv',
        'L0_cond_Wo', 'L0_cond_norm2_g', 'L0_cond_norm2_b', 'L0_cond_W1', 'L0_cond_W2', 'L0_cond_ada_W',
        'L0_cond_ada_b']


def rope_table():
    dim = np.arange(P) % D
    inv_freq = (1.0 / 10000.0 ** (np.arange(0, D, 2, dtype=np.float32) / D)).astype(np.float32)
    t, i = np.meshgrid(np.arange(T), np.arange(I), indexing="ij")
    pos = (T * i + t).reshape(-1).astype(np.float32)
    angle = (pos[None, :] * inv_freq[dim % (D // 2)][:, None]).astype(np.float32)
    sign = np.where(dim < D // 2, -1.0, 1.0).astype(np.float32)[:, None]
    table = np.stack([np.cos(angle), sign * np.sin(angle)], axis=1) * ROPE_SCALE
    head = np.arange(P) // D
    parity = np.stack([head % 2 == 0, head % 2 == 1], axis=1)
    return np.ascontiguousarray(np.concatenate([table.reshape(P, 2 * N), parity], axis=1).astype(np.float32))


def kernel(**inputs):
    import concourse.bacc as _bacc
    from concourse import mybir as _mybir
    from concourse.bass_utils import run_bass_kernel_spmd as _run

    nc = _bacc.Bacc("TRN2", target_bir_lowering=False, num_devices=1)
    arrays, args = {}, []
    for name in _INS + ["rope"]:
        a = rope_table() if name == "rope" else np.ascontiguousarray(inputs[name])
        arrays[f"in_{name}_dram"] = a
        args.append(nc.dram_tensor(f"in_{name}_dram", a.shape, _mybir.dt.from_np(a.dtype), kind="ExternalInput").ap())
    args.append(nc.dram_tensor("out_0_dram", (B, N, C), F32, kind="ExternalOutput").ap())
    build(nc, *args)
    r = _run(nc, [arrays], core_ids=[0])
    return r.results[0]["out_0_dram"]
```

```python
from contextlib import ExitStack

import numpy as np

import concourse.bass as bass
from concourse import mybir

F32 = mybir.dt.float32
F16 = mybir.dt.float16
ALU = mybir.AluOpType
ACT = mybir.ActivationFunctionType
AX_X = mybir.AxisListType.X

P = 128
B, N, C = 128, 64, 256
H, D = 16, 16
F = 4 * C
KT = C // P
GB = 8
G = B // GB
T = 4
I = P // GB
GT = GB * N
J = H // 2
JK = J // KT
BP = GB // 2
FU = F // P
D1 = D + 1
EPS = 1e-5

W_SCALE = 64.0
V_SCALE = 4.0
X_SCALE = 16.0
QK_SCALE = 4.0
ROPE_SCALE = QK_SCALE / (W_SCALE * X_SCALE)
EXP_SCALE = D ** -0.5 / (QK_SCALE * QK_SCALE)
MAX_SCALE = QK_SCALE * QK_SCALE
O_SCALE = V_SCALE * X_SCALE
GATE1_SCALE = 1.0 / (O_SCALE * W_SCALE)
GATE2_SCALE = 1.0 / W_SCALE
GELU_SCALE = 1.0 / (W_SCALE * X_SCALE)


def build(nc, x, cond, g1, b1, wq, wk, wv, wo, g2, b2, w1, w2, ada_w, ada_b, rope, out):
    ctx = ExitStack()
    with ctx:
        def sb(name, shape, dt):
            return ctx.enter_context(nc.sbuf_tensor(name, shape, dt))

        def psum(name, shape, dt):
            return ctx.enter_context(nc.psum_tensor(name, shape, dt))

        def sem(name):
            return ctx.enter_context(nc.semaphore(name))

        x_g = x.rearrange("(g b) (i t) c -> g (b i) (t c)", b=GB, t=T)
        out_g = out.rearrange("(g b) (i t) c -> g (b i) (t c)", b=GB, t=T)
        mod_dram = nc.dram_tensor("mod_scratch", (B, 6, C), F32).ap()
        mod_g = mod_dram.rearrange("(g b) s c -> g b s c", b=GB)

        w_qk = sb("w_qk", [P, 2, 2, KT, C], F16)
        w_v = sb("w_v", [P, 2, KT, C], F16)
        w_o = sb("w_o", [P, 2, KT, C], F16)
        w_1 = sb("w_1", [P, 2, KT, F], F16)
        w_2 = sb("w_2", [P, 2, FU, C], F16)
        ident16 = sb("ident16", [P, P], F16)
        ident32 = sb("ident32", [P, P], F32)
        table = sb("table", [P, 2 * N + 2], F32)
        rope_sb = table[:, 0:2 * N].rearrange("p (s n) -> p s n", s=2)
        parity = table[:, 2 * N:2 * N + 2]
        table_probe = sb("table_probe", [P, 1], F32)
        minus_half = sb("minus_half", [P, T], F32)
        selector_row = sb("selector_row", [2, 2 * N], F16)

        x_in = sb("x_in", [P, T, C], F32)
        x_res = sb("x_res", [P, T, C], F32)
        x_mid = sb("x_mid", [P, T, C], F32)
        x_late = sb("x_late", [P, T, C], F32)
        out_sb = sb("out_sb", [P, T, C], F32)
        mod1 = sb("mod1", [P, 2, C], F32)
        mod2 = sb("mod2", [P, 3, C], F32)
        mod3 = sb("mod3", [P, 1, C], F32)
        stats = sb("stats", [P, 2, T, 6], F32)
        moments = sb("moments", [P, 2, T, 2], F32)
        var_eps = sb("var_eps", [P, 2, T], F32)
        rstd = sb("rstd", [P, 2, T], F32)
        n1_32 = sb("n1_32", [P, T, C], F32)
        n1_16 = sb("n1_16", [P, T, 2, C], F16)
        n2_32 = sb("n2_32", [P, T, C], F32)
        n2_16 = sb("n2_16", [P, T, 2, C], F16)
        n1T = sb("n1T", [P, 2, KT, GT], F16)
        n2T = sb("n2T", [P, 2, KT, GT], F16)
        rope_s = sb("rope_s", [P, 4, GT], F32)
        qk_32 = sb("qk_32", [P, 4, GT], F32)
        q_16 = sb("q_16", [P, KT, 2, GT], F16)
        k_16 = sb("k_16", [P, KT, 2, GB, 2, N], F16)
        q_stack = sb("q_stack", [P, J, GT], F16)
        k_stack = sb("k_stack", [P, J, GB, 2, N], F16)
        v_16 = sb("v_16", [P, BP, 2, 2, J, D1], F16)
        v_diag = sb("v_diag", [P, GB, 2, 2, J, D1], F16)
        smax = sb("smax", [P, BP, H], F32)
        smaxT = sb("smaxT", [H, GT], F16)
        p_32 = sb("p_32", [P, 4, J * N], F32)
        p_16 = sb("p_16", [P, 4, 2, J * N], F16)
        rsum = sb("rsum", [P, BP, H], F32)
        o_32 = sb("o_32", [P, 2, C], F32)
        o_16 = sb("o_16", [P, BP, 2, C], F16)
        oT = sb("oT", [P, 2, KT, GT], F16)
        gated = sb("gated", [P, T + 2, C], F32)
        h_32 = sb("h_32", [P, 3, GT], F32)
        h_16 = sb("h_16", [P, FU, 2, GT], F16)

        ps_proj = [psum(f"ps_proj{n}", [P, GT], F32) for n in range(2)]
        ps_tok = [psum(f"ps_tok{n}", [P, 512], F32)[:, 0:C] for n in range(2)]
        ps_score = [psum(f"ps_score{n}", [P, 512], F32) for n in range(2)]
        ps_turn = [ps[:, 0:C].bitcast(F16).rearrange("p (h k n) -> p h k n", h=2, k=KT) for ps in ps_score]
        ps_pv = [psum(f"ps_pv{n}", [P, 512], F32) for n in range(2)]
        pv_out = [ps[:, 0:J * 2 * D1].rearrange("p (h e) -> p h e", e=D1) for ps in ps_pv]
        ps_smaxT = [ps[0:H, 384:384 + P] for ps in ps_pv]

        stage_h = h_16[:].rearrange("p u a n -> p (u a n)").bitcast(F32)
        stage_w1 = stage_h[:, 0:KT * F].rearrange("p (k n) -> p k n", k=KT)
        stage_w2 = stage_h[:, KT * F:KT * F + FU * C].rearrange("p (u n) -> p u n", u=FU)
        stage_q = q_stack[:].rearrange("p j n -> p (j n)").bitcast(F32)
        stage_qkvo = stage_q.rearrange("p (w k n) -> p w k n", w=4, k=KT)
        stage_ada_a = p_32[:].rearrange("p a n -> p (a n)").rearrange("p (k n) -> p k n", k=KT)
        stage_ada_b = x_mid[:].rearrange("p t c -> p (t c)").rearrange("p (k n) -> p k n", k=KT)
        stage_norm = x_late
        stage_mod = oT[:].rearrange("p h k n -> p (h k n)").bitcast(F32)
        stage_mod = stage_mod.rearrange("p (s n) -> p s n", n=C)
        stage_mod2 = out_sb[:, 0:2]

        def mod_row(s):
            return stage_mod[:, s] if s < 4 else stage_mod2[:, s - 4]

        mod_out = p_16[:].rearrange("p a h n -> p (a h n)").bitcast(F32)[:, 0:6 * C]
        mod_out = mod_out.rearrange("p (s n) -> p s n", s=6)
        cond_sb = n1_32[:, 0, :]
        cond_e = n1_32[:, 1, :]
        cond_r = n1_32[:, 2, :]
        cond_s = n1_32[:, 3, :]
        condT = n2_32[:, 0, :].rearrange("p (k b) -> p k b", k=KT)
        ada_b_sb = h_32[:].rearrange("p a n -> p (a n)")[:, 0:6 * C].rearrange("p (s n) -> p s n", s=6)

        cond_in = sem("cond_in")
        ada1_in = sem("ada1_in")
        ada2_in = sem("ada2_in")
        wqkvo_in = sem("wqkvo_in")
        wmlp_in = sem("wmlp_in")
        rope_in = sem("rope_in")
        zeroed = sem("zeroed")
        ident_done = sem("ident_done")
        cond_exp = sem("cond_exp")
        cond_step = sem("cond_step")
        condT_ps = sem("condT_ps")
        condT_done = sem("condT_done")
        mod_ps = sem("mod_ps")
        mod1_step = sem("mod1_step")
        mod2_step = sem("mod2_step")
        mod1_stored = sem("mod1_stored")
        mod_stored = sem("mod_stored")
        w_hi = sem("w_hi")
        w_lo = sem("w_lo")
        stacks_clear = sem("stacks_clear")
        selector = sem("selector")
        selector_set = sem("selector_set")

        x_loaded = sem("x_loaded")
        x_res_loaded = sem("x_res_loaded")
        x_late_copied = sem("x_late_copied")
        mod1_loaded = sem("mod1_loaded")
        mod2_loaded = sem("mod2_loaded")
        mod3_loaded = sem("mod3_loaded")
        ln1_stats = sem("ln1_stats")
        ln1_var = sem("ln1_var")
        ln1_rstd = sem("ln1_rstd")
        ln1_factor = sem("ln1_factor")
        ln1_done = sem("ln1_done")
        ln1_hi = sem("ln1_hi")
        ln1_lo = sem("ln1_lo")
        ln2_stats = sem("ln2_stats")
        ln2_var = sem("ln2_var")
        ln2_rstd = sem("ln2_rstd")
        ln2_factor = sem("ln2_factor")
        ln2_done = sem("ln2_done")
        ln2_hi = sem("ln2_hi")
        ln2_lo = sem("ln2_lo")
        n1_turned = sem("n1_turned")
        n2_turned = sem("n2_turned")
        o_turned = sem("o_turned")
        n1_out = sem("n1_out")
        n2_out = sem("n2_out")
        o_part = sem("o_part")
        o_out = sem("o_out")
        qk_ps = sem("qk_ps")
        rope_half = sem("rope_half")
        rope_sin = sem("rope_sin")
        rope_sum = sem("rope_sum")
        last_sin = sem("last_sin")
        last_sum = sem("last_sum")
        qk_hi = sem("qk_hi")
        qk_lo = sem("qk_lo")
        v_ps = sem("v_ps")
        v_hi = sem("v_hi")
        v_lo = sem("v_lo")
        hi_stacked = sem("hi_stacked")
        lo_stacked = sem("lo_stacked")
        hi_doubled = sem("hi_doubled")
        v_stacked = sem("v_stacked")
        s_ps = sem("s_ps")
        smax_done = sem("smax_done")
        smaxT_ps = sem("smaxT_ps")
        smaxT_done = sem("smaxT_done")
        smax_stacked = [sem(f"smax_stacked{n}") for n in range(2)]
        st_ps = sem("st_ps")
        exp_done = sem("exp_done")
        p_hi = sem("p_hi")
        p_lo = [sem(f"p_lo{n}") for n in range(2)]
        pv_ps = sem("pv_ps")
        rsum_done = sem("rsum_done")
        o_done = sem("o_done")
        o_hi = sem("o_hi")
        o_lo = sem("o_lo")
        attn_ps = sem("attn_ps")
        gated1 = sem("gated1")
        mid_done = sem("mid_done")
        h_ps = sem("h_ps")
        gelu_done = sem("gelu_done")
        h_hi = sem("h_hi")
        h_lo = [sem(f"h_lo{n}") for n in range(2)]
        mlp_ps = sem("mlp_ps")
        gated2 = sem("gated2")
        out_done = sem("out_done")
        stored = sem("stored")
        table_loaded = sem("table_loaded")

        block = ctx.enter_context(nc.Block())

        def is_first(g):
            return isinstance(g, int) and g == 0

        def tok_v(q):
            return ps_tok[(q + q // 2) % 2]

        def tok_wo(t):
            return ps_tok[t % 2]

        def tok_mlp(t):
            return ps_tok[t % 2]

        def gated_wo(t):
            return gated[:, t]

        def gated_mlp(t):
            return gated[:, T + t % 2]

        STACK_COUNT = 16 * 2 * J
        P_LOW_DVE, P_LOW_POOL = (0, 2, 4, 6, 7), (1, 3, 5)

        def p_low_made(g, b):
            n = b in P_LOW_POOL
            batches = P_LOW_POOL if n else P_LOW_DVE
            return p_lo[n], g * len(batches) + batches.index(b) + 1

        def p_low_made_before(g, b):
            n = b in P_LOW_POOL
            batches = P_LOW_POOL if n else P_LOW_DVE
            return p_lo[n], g * len(batches) - (len(batches) - batches.index(b) - 1)

        @block.sync
        def _(sp):
            sp.dma_start(cond_sb, cond).then_inc(cond_in, 16)
            ada_w_k = ada_w.rearrange("(k p) n -> p k n", p=P)
            sp.dma_start(stage_ada_a[:, :, 0:2 * C], ada_w_k[:, :, 0:2 * C]).then_inc(ada1_in, 16)
            sp.dma_start(ada_b_sb.rearrange("p s n -> p (s n)"), ada_b.partition_broadcast(P)).then_inc(ada1_in, 16)
            for n, v in enumerate((g1, b1)):
                sp.dma_start(stage_norm[:, n, :], v.partition_broadcast(P)).then_inc(ada1_in, 16)
            sp.dma_start(x_in[:].rearrange("p t c -> p (t c)"), x_g[0]).then_inc(x_loaded, 16)
            for n, w in enumerate((wq, wk, wv, wo)):
                sp.dma_start(stage_qkvo[:, n], w.rearrange("(k p) n -> p k n", p=P)).then_inc(wqkvo_in, 16)
            sp.dma_start(table[:], rope).then_inc(rope_in, 16)
            sp.wait_ge(mod1_step, 6)
            sp.dma_start(mod_dram[:, 0:2], mod_out[:, 0:2]).then_inc(mod1_stored, 16)
            sp.wait_ge(mod1_stored, 16)
            sp.dma_start(mod1[:].rearrange("p s c -> p (s c)"),
                         mod_g[0][:, 0:2, :].rearrange("b s c -> b (s c)").unsqueeze(1).to_broadcast([GB, I, 2 * C])
                         ).then_inc(mod1_loaded, 16)
            sp.dma_start(stage_ada_a[:, :, 2 * C:4 * C], ada_w_k[:, :, 2 * C:4 * C]).then_inc(ada2_in, 16)
            sp.dma_start(stage_ada_b, ada_w_k[:, :, 4 * C:6 * C]).then_inc(ada2_in, 16)
            for n, v in enumerate((g2, b2)):
                sp.dma_start(stage_norm[:, 2 + n, :], v.partition_broadcast(P)).then_inc(ada2_in, 16)
            sp.dma_start(stage_w1, w1.rearrange("(k p) n -> p k n", p=P)).then_inc(wmlp_in, 16)
            sp.dma_start(stage_w2, w2.rearrange("(u p) n -> p u n", p=P)).then_inc(wmlp_in, 16)

            def load_mod(dst, g, s0, s1, done):
                sp.wait_ge(mod1_stored, 16)
                src = mod_g[g][:, s0:s1, :].rearrange("b s c -> b (s c)")
                rows = src.unsqueeze(1).to_broadcast([GB, I, (s1 - s0) * C])
                sp.dma_start(dst.rearrange("p s c -> p (s c)"), rows).then_inc(done, 16)

            def restack(i):
                for qk, kt, part in ((0, 0, 0), (0, 0, 1), (0, 1, 0), (0, 1, 1), (1, 0, 0), (1, 1, 0), (1, 0, 1), (1, 1, 1)):
                    src, stack = (q_16, q_stack) if qk == 0 else (k_16, k_stack)
                    row = 32 * ((0, 2), (0, 1))[qk][part]
                    sp.wait_ge((qk_hi, qk_lo)[part], i * 8 + 4 * qk + 2 * kt + 2)
                    if part == qk == kt == 0 and not is_first(i):
                        sp.wait_ge(st_ps, i * GB)
                    for j in range(JK):
                        sp.dma_start(stack[row:row + 32, JK * kt + j],
                                     src[32 * j:32 * j + 32, kt, part]).then_inc((hi_stacked, lo_stacked)[part], 16)

            def restack_v(i):
                sp.wait_ge(v_hi, i * BP + BP)
                sp.wait_ge(v_lo, i * BP + BP)
                for a in range(2):
                    for b in range(2):
                        src = v_16[N * b:N * b + N, :, a].rearrange("m q h j e -> m q (h j e)")
                        dst = v_diag[N * a:N * a + N, b:GB:2, a].rearrange("m q h j e -> m q (h j e)")
                        sp.dma_start(dst, src).then_inc(v_stacked, 16)

            def stack_max(i, half):
                sp.wait_ge(smaxT_done, i * BP + 2 * half + 2)
                cols = slice(half * 2 * P, half * 2 * P + 2 * P)
                for a in range(2):
                    src = smaxT[a:H:2, cols]
                    sp.dma_start(q_stack[96 + a:97 + a, :, cols], src).then_inc(smax_stacked[half], 16)

            def iteration(i, project, attend, mlp2, norm_next):
                if attend:
                    if not is_first(i - 1):
                        sp.wait_ge(mid_done, (i - 1) * T)
                        sp.wait_ge(ln2_done, (i - 1) * T)
                        sp.wait_ge(mod1_stored, 16)
                    sp.dma_start(x_res[:].rearrange("p t c -> p (t c)"), x_g[i - 1]).then_inc(x_res_loaded, 16)
                    load_mod(mod2[:], i - 1, 2, 5, mod2_loaded)
                if mlp2:
                    if not is_first(i - 2):
                        sp.wait_ge(gated2, (i - 2) * T)
                    load_mod(mod3[:], i - 2, 5, 6, mod3_loaded)
                if norm_next:
                    sp.wait_ge(ln1_done, i * T + T)
                    sp.wait_ge(mod1_stored, 16)
                    sp.dma_start(x_in[:].rearrange("p t c -> p (t c)"), x_g[i + 1]).then_inc(x_loaded, 16)
                    load_mod(mod1[:], i + 1, 0, 2, mod1_loaded)
                if attend:
                    stack_max(i - 1, 0)
                    stack_max(i - 1, 1)
                if project:
                    restack(i)
                    if not is_first(i):
                        sp.wait_ge(pv_ps, i * BP)
                    restack_v(i)
                if mlp2:
                    sp.wait_ge(out_done, (i - 1) * T)
                    sp.wait_ge(mod1_stored, 16)
                    sp.dma_start(out_g[i - 2], out_sb[:].rearrange("p t c -> p (t c)")).then_inc(stored, 16)
                if attend:
                    sp.wait_ge(mid_done, i * T)
                    sp.dma_start(x_late[:], x_mid[:]).then_inc(x_late_copied, 16)

            sp.wait_ge(stacks_clear, 4)
            sp.wait_ge(selector, 1)
            sp.dma_start(k_stack[96:98].rearrange("p j b a n -> p (j b) (a n)"),
                         selector_row[:].unsqueeze(1).to_broadcast([2, J * GB, 2 * N])).then_inc(selector_set, 16)
            sp.wait_ge(selector_set, 16)
            iteration(0, True, False, False, True)
            sp.wait_ge(mod2_step, 9)
            sp.dma_start(mod_dram[:, 2:6], mod_out[:, 2:6]).then_inc(mod_stored, 16)
            sp.wait_ge(mod_stored, 16)
            iteration(1, True, True, False, True)
            iteration(2, True, True, True, True)
            with sp.Fori(3, G - 1) as i:
                iteration(i, True, True, True, True)
            iteration(G - 1, True, True, True, False)
            iteration(G, False, True, True, False)
            iteration(G + 1, False, False, True, False)
            sp.wait_ge(stored, 16 * G)

        @block.gpsimd
        def _(pool):
            pool.memset(minus_half[:], -0.5).then_inc(zeroed, 1)
            pool.memset(ident16[:], 0.0).then_inc(zeroed, 1)
            pool.memset(ident32[:], 0.0).then_inc(zeroed, 1)
            pool.wait_ge(zeroed, 3)
            for m in (ident16, ident32):
                pool.affine_select(out=m[:], in_=m[:], compare_op=ALU.not_equal, fill=1.0, base=0,
                                   pattern=[[-1, P]], channel_multiplier=1).then_inc(ident_done, 1)
            pool.memset(v_16[:, :, :, 0, :, D:D1].rearrange("p q a j e -> p (q a) (j e)"), 1.0).then_inc(stacks_clear, 1)
            pool.memset(v_16[:, :, :, 1, :, D:D1].rearrange("p q a j e -> p (q a) (j e)"), 0.0).then_inc(stacks_clear, 1)
            pool.memset(v_diag[:].rearrange("p b a h j e -> p (b a h j e)"), 0.0).then_inc(stacks_clear, 1)
            pool.memset(k_stack[:].rearrange("p j b a n -> p (j b a n)"), 0.0).then_inc(stacks_clear, 1)
            pool.memset(selector_row[:], 0.0).then_inc(zeroed, 1)
            pool.wait_ge(zeroed, 4)
            sel = selector_row[:].rearrange("p (a n) -> p a n", a=2)
            pool.affine_select(out=sel, in_=sel, compare_op=ALU.not_equal, fill=-MAX_SCALE, base=0,
                               pattern=[[-1, 2], [0, N]], channel_multiplier=1).then_inc(selector, 1)

            def norm_rstd(k, g, var, done):
                pool.wait_ge(var, g + 1)
                pool.tensor_tensor(rstd[:, k], var_eps[:, k], minus_half[:], ALU.pow).then_inc(done, 1)

            def norm_lo(g, n32, n16, hi, lo):
                for t in range(T):
                    pool.wait_ge(hi, g * T + t + 1)
                    pool.tensor_tensor(n16[:, t, 1], n32[:, t], n16[:, t, 0], ALU.subtract).then_inc(lo, 1)

            def rotary_sin(i, c):
                pool.wait_ge(rope_half, i * 8 + 2 * c + 2)
                turned = rope_s[:, c].rearrange("p (b n) -> p b n", b=GB)
                pool.tensor_tensor(turned, turned, rope_sb[:, 1].unsqueeze(1).to_broadcast([P, GB, N]),
                                   ALU.mult).then_inc(rope_sin, 1)

            def rotary_sum(i, c):
                pool.wait_ge(rope_sin, i * 3 + c + 1)
                pool.tensor_tensor(qk_32[:, c], qk_32[:, c], rope_s[:, c], ALU.add).then_inc(rope_sum, 1)

            def q_low(i, c):
                pool.wait_ge(qk_hi, i * 8 + 2 * c + 2)
                if c == 0 and not is_first(i):
                    pool.wait_ge(lo_stacked, i * STACK_COUNT)
                pool.tensor_tensor(q_16[:, c, 1], qk_32[:, c], q_16[:, c, 0], ALU.subtract).then_inc(qk_lo, 2)

            def o_low(g, q):
                pool.wait_ge(o_hi, g * BP + q + 1)
                pool.tensor_tensor(o_16[:, q, 1], o_32[:, q % 2], o_16[:, q, 0], ALU.subtract).then_inc(o_lo, 1)

            def p_low(g, b):
                pool.wait_ge(p_hi, g * GB + b + 1)
                pool.tensor_tensor(p_16[:, b % 4, 1], p_32[:, b % 4], p_16[:, b % 4, 0], ALU.subtract).then_inc(p_lo[1], 1)

            def h_low(g, u):
                pool.wait_ge(h_hi, g * FU + u + 1)
                pool.tensor_tensor(h_16[:, u, 1], h_32[:, u % 3], h_16[:, u, 0], ALU.subtract).then_inc(h_lo[1], 1)

            def residual_2(g, t):
                pool.wait_ge(gated2, g * T + t + 1)
                if t == 0:
                    pool.wait_ge(x_late_copied, g * 16 + 16)
                    if not is_first(g):
                        pool.wait_ge(stored, g * 16)
                pool.tensor_tensor(out_sb[:, t], gated_mlp(t), x_late[:, t], ALU.add).then_inc(out_done, 1)

            def iteration(i, project, attend, mlp2, norm_next):
                if project:
                    rotary_sin(i, 0)
                    rotary_sum(i, 0)
                    q_low(i, 0)
                    rotary_sin(i, 1)
                if attend:
                    p_low(i - 1, 1)
                if project:
                    rotary_sum(i, 1)
                if attend:
                    p_low(i - 1, 3)
                if project:
                    q_low(i, 1)
                if attend:
                    p_low(i - 1, 5)
                    o_low(i - 1, 0)
                if project:
                    rotary_sin(i, 2)
                if attend:
                    o_low(i - 1, 1)
                if project:
                    rotary_sum(i, 2)
                if attend:
                    o_low(i - 1, 2)
                    o_low(i - 1, 3)
                if mlp2:
                    residual_2(i - 2, 0)
                if attend:
                    for t in range(T):
                        pool.wait_ge(gated1, (i - 1) * T + t + 1)
                        if t == 0:
                            pool.wait_ge(x_res_loaded, i * 16)
                            if not is_first(i - 1):
                                pool.wait_ge(x_late_copied, (i - 1) * 16)
                        pool.tensor_tensor(x_mid[:, t], gated_wo(t), x_res[:, t], ALU.add).then_inc(mid_done, 1)
                    norm_rstd(1, i - 1, ln2_var, ln2_rstd)
                if norm_next:
                    norm_rstd(0, i + 1, ln1_var, ln1_rstd)
                if attend:
                    norm_lo(i - 1, n2_32, n2_16, ln2_hi, ln2_lo)
                if mlp2:
                    residual_2(i - 2, 1)
                if norm_next:
                    norm_lo(i + 1, n1_32, n1_16, ln1_hi, ln1_lo)
                if mlp2:
                    residual_2(i - 2, 2)
                    residual_2(i - 2, 3)
                if attend:
                    for u in range(1, FU, 2):
                        h_low(i - 1, u)

            norm_rstd(0, 0, ln1_var, ln1_rstd)
            norm_lo(0, n1_32, n1_16, ln1_hi, ln1_lo)
            iteration(0, True, False, False, True)
            iteration(1, True, True, False, True)
            iteration(2, True, True, True, True)
            with pool.Fori(3, G - 1) as i:
                iteration(i, True, True, True, True)
            iteration(G - 1, True, True, True, False)
            iteration(G, False, True, True, False)
            iteration(G + 1, False, False, True, False)

        @block.scalar
        def _(act):
            act.wait_ge(cond_in, 16)
            act.activation(cond_e, cond_sb, ACT.Exp, scale=-1.0).then_inc(cond_exp, 1)
            act.wait_ge(condT_ps, 1)
            act.activation(condT, ps_score[0][:, 0:C].rearrange("p (k b) -> p k b", k=KT), ACT.Copy).then_inc(condT_done, 1)
            act.wait_ge(wqkvo_in, 64)
            for n in range(2):
                act.activation(w_qk[:, 0, n], stage_qkvo[:, n], ACT.Copy, scale=W_SCALE).then_inc(w_hi, 1)
            for kt in range(KT):
                act.activation(w_v[:, 0, kt].rearrange("p (a j r) -> p a j r", a=2, r=D),
                               stage_qkvo[:, 2, kt].rearrange("p (j a r) -> p a j r", a=2, r=D),
                               ACT.Copy, scale=V_SCALE).then_inc(w_hi, 1)
            act.activation(w_o[:, 0], stage_qkvo[:, 3], ACT.Copy, scale=W_SCALE).then_inc(w_hi, 1)

            def norm_hi(g, n32, n16, done, hi, t0=0, t1=T):
                for t in range(t0, t1):
                    act.wait_ge(done, g * T + t + 1)
                    act.activation(n16[:, t, 0], n32[:, t], ACT.Copy).then_inc(hi, 1)

            def q_k_high(i, c):
                if c < 3:
                    act.wait_ge(rope_sum, i * 3 + c + 1)
                else:
                    act.wait_ge(last_sum, i + 1)
                if c == 0 and not is_first(i):
                    act.wait_ge(hi_stacked, i * STACK_COUNT)
                    act.wait_ge(lo_stacked, i * STACK_COUNT)
                if c < 2:
                    act.activation(q_16[:, c, 0], qk_32[:, c], ACT.Copy).then_inc(qk_hi, 2)
                else:
                    for a in range(2):
                        act.activation(k_16[:, c - 2, 0, :, a], qk_32[:, c].rearrange("p (b n) -> p b n", n=N),
                                       ACT.Identity, scale=parity[:, a:a + 1]).then_inc(qk_hi, 1)

            def v_high(i, q):
                act.wait_ge(v_ps, i * BP + q + 1)
                if q == 0 and not is_first(i):
                    act.wait_ge(v_stacked, i * 64)
                act.activation(v_16[:, q, :, 0, :, 0:D], tok_v(q).rearrange("p (a j r) -> p a j r", a=2, r=D),
                               ACT.Copy).then_inc(v_hi, 1)

            def max_out(g, q):
                act.wait_ge(smaxT_ps, g * BP + q + 1)
                if q == 0 and not is_first(g):
                    for half in range(2):
                        act.wait_ge(smax_stacked[half], g * 32)
                act.activation(smaxT[:, q * P:q * P + P], ps_smaxT[q % 2], ACT.Copy,
                               scale=1.0 / MAX_SCALE).then_inc(smaxT_done, 1)

            def soft_exp(g, b):
                act.wait_ge(st_ps, g * GB + b + 1)
                if b >= 4:
                    act.wait_ge(*p_low_made(g, b - 4))
                elif not is_first(g):
                    act.wait_ge(*p_low_made_before(g, b + 4))
                act.activation(p_32[:, b % 4], ps_score[b % 2][:], ACT.Exp, scale=EXP_SCALE).then_inc(exp_done, 1)

            def p_high(g, b):
                act.wait_ge(exp_done, g * GB + b + 1)
                if b % 2 == 0 and (b >= 4 or not is_first(g)):
                    act.wait_ge(pv_ps, g * BP + b // 2 - 1)
                act.activation(p_16[:, b % 4, 0], p_32[:, b % 4], ACT.Copy).then_inc(p_hi, 1)

            def load_table(func):
                act.activation(table_probe[:], parity[:, 0:1], func).then_inc(table_loaded, 1)

            def n2_copy_out(g, t):
                act.wait_ge(n2_turned, g * T + t + 1)
                act.activation(n2T[:, :, :, t * P:t * P + P].rearrange("p h k n -> p (h k) n"),
                               ps_turn[t % 2].rearrange("p h k n -> p (h k) n"), ACT.Copy).then_inc(n2_out, 1)

            def gelu(g, u):
                act.wait_ge(h_ps, g * FU + u + 1)
                if u == 0 and not is_first(g):
                    for n in range(2):
                        act.wait_ge(h_lo[n], g * (FU // 2))
                elif u >= 3:
                    act.wait_ge(h_lo[(u - 3) % 2], g * (FU // 2) + (u - 3) // 2 + 1)
                act.activation(h_32[:, u % 3], ps_proj[u % 2][:], ACT.Gelu, scale=GELU_SCALE).then_inc(gelu_done, 1)

            def h_high(g, u):
                act.wait_ge(gelu_done, g * FU + u + 1)
                if u == 0 and not is_first(g):
                    act.wait_ge(mlp_ps, g * T)
                act.activation(h_16[:, u, 0], h_32[:, u % 3], ACT.Copy).then_inc(h_hi, 1)

            def o_high(g, q):
                act.wait_ge(o_done, g * BP + q + 1)
                act.activation(o_16[:, q, 0], o_32[:, q % 2], ACT.Copy).then_inc(o_hi, 1)

            def o_copy_out(g, q):
                act.wait_ge(o_turned, g * BP + q + 1)
                for b in range(2):
                    src = ps_turn[q % 2].rearrange("p h k (b t i) -> p (h k) b t i", b=2, i=I)[:, :, b]
                    dst = oT[:].rearrange("p h k (t b i) -> p (h k) b t i", t=T, i=I)[:, :, 2 * q + b]
                    act.activation(dst, src, ACT.Copy).then_inc(o_part if b == 0 else o_out, 1)

            def iteration(i, project, attend, mlp2, norm_next):
                g = i - 1

                def softmax_pair(b):
                    if attend:
                        soft_exp(g, b)
                        soft_exp(g, b + 1)
                        p_high(g, b)
                        p_high(g, b + 1)

                if attend:
                    max_out(g, 0)
                    max_out(g, 1)
                if project:
                    q_k_high(i, 0)
                if attend:
                    max_out(g, 2)
                    max_out(g, 3)
                if project:
                    v_high(i, 0)
                softmax_pair(0)
                if attend:
                    soft_exp(g, 2)
                    soft_exp(g, 3)
                if project:
                    v_high(i, 1)
                if attend:
                    p_high(g, 2)
                    p_high(g, 3)
                    soft_exp(g, 4)
                    soft_exp(g, 5)
                if project:
                    q_k_high(i, 1)
                if attend:
                    p_high(g, 4)
                    p_high(g, 5)
                    o_high(g, 0)
                softmax_pair(6)
                if project:
                    v_high(i, 2)
                if attend:
                    o_high(g, 1)
                    o_copy_out(g, 0)
                    o_high(g, 2)
                    o_copy_out(g, 1)
                    o_high(g, 3)
                if project:
                    v_high(i, 3)
                if attend:
                    o_copy_out(g, 2)
                    o_copy_out(g, 3)
                if project:
                    q_k_high(i, 2)
                    q_k_high(i, 3)
                if attend:
                    load_table(ACT.Gelu)
                    norm_hi(g, n2_32, n2_16, ln2_done, ln2_hi)
                    for t in range(T):
                        n2_copy_out(g, t)
                    gelu(g, 0)
                if norm_next:
                    norm_hi(i + 1, n1_32, n1_16, ln1_done, ln1_hi, 0, 1)
                if attend:
                    gelu(g, 1)
                if norm_next:
                    norm_hi(i + 1, n1_32, n1_16, ln1_done, ln1_hi, 1, T)
                if attend:
                    h_high(g, 0)
                    for u in range(2, FU):
                        gelu(g, u)
                        h_high(g, u - 1)
                    h_high(g, FU - 1)
                    if project:
                        load_table(ACT.Exp)

            norm_hi(0, n1_32, n1_16, ln1_done, ln1_hi)
            act.wait_ge(wmlp_in, 32)
            act.activation(w_1[:, 0], stage_w1, ACT.Copy, scale=W_SCALE).then_inc(w_hi, 1)
            act.activation(w_2[:, 0], stage_w2, ACT.Copy, scale=W_SCALE).then_inc(w_hi, 1)
            act.wait_ge(rope_in, 16)
            iteration(0, True, False, False, True)
            iteration(1, True, True, False, True)
            iteration(2, True, True, True, True)
            with act.Fori(3, G - 1) as i:
                iteration(i, True, True, True, True)
            iteration(G - 1, True, True, True, False)
            iteration(G, False, True, True, False)
            iteration(G + 1, False, False, True, False)

        @block.vector
        def _(dve):
            dve.wait_ge(cond_exp, 1)
            dve.tensor_scalar(cond_e, cond_e, 1.0, None, ALU.add).then_inc(cond_step, 1)
            dve.wait_ge(cond_step, 1)
            dve.reciprocal(cond_r, cond_e).then_inc(cond_step, 1)
            dve.wait_ge(cond_step, 2)
            dve.tensor_tensor(cond_s, cond_sb, cond_r, ALU.mult).then_inc(cond_step, 1)

            def norm_stat(k, g, src, t, in_done, in_count, stats_done):
                if in_count is not None:
                    dve.wait_ge(in_done, in_count)
                dve.bn_stats(stats[:, k, t], src[:, t]).then_inc(stats_done, 1)

            def norm_var(k, g, stats_done, var_done):
                dve.wait_ge(stats_done, g * (2 * T + 1) + T)
                dve.memset(var_eps[:, k], EPS).then_inc(stats_done, 1)
                for t in range(T):
                    dve.bn_aggr(moments[:, k, t], stats[:, k, t]).then_inc(stats_done, 1)
                dve.wait_ge(stats_done, g * (2 * T + 1) + 2 * T + 1)
                dve.tensor_tensor(var_eps[:, k], moments[:, k, :, 1], var_eps[:, k], ALU.add).then_inc(var_done, 1)

            def norm_factor(k, g, src, mod, m0, n32, factor, t0=0, t1=T):
                for t in range(t0, t1):
                    dve.scalar_tensor_tensor(n32[:, t], src[:, t], moments[:, k, t, 0:1], mod[:, m0],
                                             ALU.subtract, ALU.mult).then_inc(factor, 1)

            def norm_shift(k, g, mod, m0, n32, factor, rstd_done, done, t0=0, t1=T):
                dve.wait_ge(rstd_done, g + 1)
                for t in range(t0, t1):
                    dve.wait_ge(factor, g * T + t + 1)
                    dve.scalar_tensor_tensor(n32[:, t], n32[:, t], rstd[:, k, t:t + 1], mod[:, m0 + 1],
                                             ALU.mult, ALU.add).then_inc(done, 1)

            def norm1_stat(g, t):
                norm_stat(0, g, x_in, t, x_loaded, g * 16 + 16 if t == 0 else None, ln1_stats)

            def norm1_factor(g):
                dve.wait_ge(mod1_loaded, g * 16 + 16)
                if not is_first(g):
                    dve.wait_ge(ln1_lo, g * T)
                norm_factor(0, g, x_in, mod1, 0, n1_32, ln1_factor)

            def norm1_shift(g, t0=0, t1=T):
                norm_shift(0, g, mod1, 0, n1_32, ln1_factor, ln1_rstd, ln1_done, t0, t1)

            def n1_copy_out(g, t):
                dve.wait_ge(n1_turned, g * T + t + 1)
                dst = n1T[:].rearrange("p h k (b t i) -> p (h k) b t i", t=T, i=I)[:, :, :, t]
                dve.tensor_copy(dst, ps_turn[t % 2].rearrange("p h k (b i) -> p (h k) b i", i=I)).then_inc(n1_out, 1)

            for t in range(T):
                norm1_stat(0, t)
            norm_var(0, 0, ln1_stats, ln1_var)

            def mod_rows(n, ps, step):
                dve.wait_ge(mod_ps, n + 1)
                dve.tensor_tensor(stage_mod[:, 2 * n:2 * n + 2] if n < 2 else stage_mod2, ps[:].rearrange("p (s c) -> p s c", s=2),
                                  ada_b_sb[:, 2 * n:2 * n + 2], ALU.add).then_inc(step, 1)

            def factor_and_shift(n, fac, sh, step, count):
                scale, shift = mod_row(3 * n + 1), mod_row(3 * n)
                dve.wait_ge(step, count)
                dve.scalar_tensor_tensor(mod_out[:, fac], scale, 1.0, stage_norm[:, 2 * n], ALU.add, ALU.mult).then_inc(step, 1)
                dve.scalar_tensor_tensor(mod_out[:, sh], scale, 1.0, stage_norm[:, 2 * n + 1], ALU.add, ALU.mult).then_inc(step, 1)
                dve.wait_ge(step, count + 2)
                dve.tensor_tensor(mod_out[:, sh], mod_out[:, sh], shift, ALU.add).then_inc(step, 1)
                dve.wait_ge(step, count + 3)
                for m in (fac, sh):
                    dve.tensor_scalar(mod_out[:, m], mod_out[:, m], X_SCALE, None, ALU.mult).then_inc(step, 1)

            dve.wait_ge(ada1_in, 16 * 4)
            mod_rows(0, ps_proj[0], mod1_step)
            factor_and_shift(0, 0, 1, mod1_step, 1)

            def low(dst, src, hi, scale, count):
                dve.wait_ge(w_hi, count)
                dve.scalar_tensor_tensor(dst, src, scale, hi, ALU.mult, ALU.subtract).then_inc(w_lo, 1)

            for n in range(2):
                low(w_qk[:, 1, n], stage_qkvo[:, n], w_qk[:, 0, n], W_SCALE, n + 1)
            for kt in range(KT):
                for a in range(2):
                    low(w_v[:, 1, kt].rearrange("p (a j r) -> p a j r", a=2, r=D)[:, a],
                        stage_qkvo[:, 2, kt].rearrange("p (j a r) -> p a j r", a=2, r=D)[:, a],
                        w_v[:, 0, kt].rearrange("p (a j r) -> p a j r", a=2, r=D)[:, a], V_SCALE, 3 + kt)
            norm1_factor(0)
            norm1_shift(0)
            for t in range(T):
                n1_copy_out(0, t)
            low(w_o[:, 1], stage_qkvo[:, 3], w_o[:, 0], W_SCALE, 5)
            dve.wait_ge(rope_in, 16)

            def late_modulation():
                dve.wait_ge(ada2_in, 16 * 4)
                mod_rows(1, ps_pv[0], mod2_step)
                mod_rows(2, ps_pv[1], mod2_step)
                factor_and_shift(1, 3, 4, mod2_step, 2)
                dve.tensor_scalar(mod_out[:, 2], mod_row(2), GATE1_SCALE, None, ALU.mult).then_inc(mod2_step, 1)
                dve.tensor_scalar(mod_out[:, 5], mod_row(5), GATE2_SCALE, None, ALU.mult).then_inc(mod2_step, 1)

            ROTATED = [D * h + (2 * j + 1) % (D + 1) for h in range(2) for j in range(D)]

            def rotary(i, c):
                dve.wait_ge(qk_ps, i * 4 + c + 1)
                if not is_first(i):
                    dve.wait_ge(qk_lo, i * 8 + 2 * c - 6)
                dve.tensor_tensor(qk_32[:, c].rearrange("p (b n) -> p b n", b=GB),
                                  ps_proj[c % 2][:].rearrange("p (b n) -> p b n", b=GB),
                                  rope_sb[:, 0].unsqueeze(1).to_broadcast([P, GB, N]), ALU.mult).then_inc(rope_half, 1)
                dve.stream_shuffle(rope_s[:, c], ps_proj[c % 2][:], ROTATED).then_inc(rope_half, 1)

            def last_rotary_sum(i):
                dve.wait_ge(rope_half, i * 8 + 8)
                turned = rope_s[:, 3].rearrange("p (b n) -> p b n", b=GB)
                dve.tensor_tensor(turned, turned, rope_sb[:, 1].unsqueeze(1).to_broadcast([P, GB, N]),
                                  ALU.mult).then_inc(last_sin, 1)
                dve.wait_ge(last_sin, i + 1)
                dve.tensor_tensor(qk_32[:, 3], qk_32[:, 3], rope_s[:, 3], ALU.add).then_inc(last_sum, 1)

            def k_low(i, c):
                dve.wait_ge(qk_hi, i * 8 + 2 * c + 2)
                for a in range(2):
                    dve.scalar_tensor_tensor(k_16[:, c - 2, 1, :, a], qk_32[:, c].rearrange("p (b n) -> p b n", n=N),
                                             parity[:, a:a + 1], k_16[:, c - 2, 0, :, a], ALU.mult,
                                             ALU.subtract).then_inc(qk_lo, 1)

            def v_low(i, q):
                dve.wait_ge(v_hi, i * BP + q + 1)
                dve.tensor_tensor(v_16[:, q, :, 1, :, 0:D], tok_v(q).rearrange("p (a j r) -> p a j r", a=2, r=D),
                                  v_16[:, q, :, 0, :, 0:D], ALU.subtract).then_inc(v_lo, 1)

            def h_low(g, u):
                dve.wait_ge(h_hi, g * FU + u + 1)
                dve.tensor_tensor(h_16[:, u, 1], h_32[:, u % 3], h_16[:, u, 0], ALU.subtract).then_inc(h_lo[0], 1)

            def score_max(g, s):
                dve.wait_ge(s_ps, g * 8 + s + 1)
                dve.tensor_reduce(smax[:, s // 2, J * (s % 2):J * (s % 2) + J],
                                  ps_score[s % 2][:].rearrange("p (h m) -> p h m", m=N), AX_X, ALU.max).then_inc(smax_done, 1)

            def p_low(g, b):
                dve.wait_ge(p_hi, g * GB + b + 1)
                dve.tensor_tensor(p_16[:, b % 4, 1], p_32[:, b % 4], p_16[:, b % 4, 0], ALU.subtract).then_inc(p_lo[0], 1)

            def attn_out(g, q):
                pv = pv_out[q % 2]
                dve.wait_ge(pv_ps, g * BP + q + 1)
                dve.reciprocal(rsum[:, q], pv[:, :, D]).then_inc(rsum_done, 1)
                dve.wait_ge(rsum_done, g * BP + q + 1)
                if q >= 2 or not is_first(g):
                    dve.wait_ge(o_lo, g * BP + q - 1)
                dve.tensor_tensor(o_32[:, q % 2].rearrange("p (h r) -> p h r", r=D), pv[:, :, 0:D],
                                  rsum[:, q].unsqueeze(2).to_broadcast([P, H, D]), ALU.mult).then_inc(o_done, 1)

            def gate_1(g, t):
                dve.wait_ge(attn_ps, g * T + t + 1)
                if t == 0:
                    dve.wait_ge(mod2_loaded, g * 16 + 16)
                dve.tensor_tensor(gated_wo(t), tok_wo(t), mod2[:, 0], ALU.mult).then_inc(gated1, 1)

            def gate_2(g, t):
                dve.wait_ge(mlp_ps, g * T + t + 1)
                if t == 0:
                    dve.wait_ge(mod3_loaded, g * 16 + 16)
                if t >= 2:
                    dve.wait_ge(out_done, g * T + t - 1)
                elif t == 0 and not is_first(g):
                    dve.wait_ge(out_done, g * T)
                dve.tensor_tensor(gated_mlp(t), tok_mlp(t), mod3[:, 0], ALU.mult).then_inc(gated2, 1)

            def double_high(i, stack, row, first):
                if first:
                    dve.wait_ge(hi_stacked, (i + 1) * STACK_COUNT)
                view = stack[:].rearrange("p j n -> p (j n)") if stack is q_stack else \
                    stack[:].rearrange("p j b a n -> p (j b a n)")
                dve.tensor_copy(view[row:row + 32], view[0:32]).then_inc(hi_doubled, 1)

            def iteration(i, project, attend, mlp2, norm_next):
                g = i - 1

                def p_lows(*bs):
                    if attend:
                        for b in bs:
                            p_low(g, b)

                def out(*qs):
                    if attend:
                        for q in qs:
                            attn_out(g, q)

                def rotaries(*us):
                    if project:
                        for u in us:
                            rotary(i, u)

                def stats1(*ts):
                    if norm_next:
                        for t in ts:
                            norm1_stat(i + 1, t)

                def maxima(*ss):
                    if attend:
                        for s in ss:
                            score_max(g, s)

                maxima(0, 1)
                if mlp2:
                    h_low(i - 2, FU - 2)
                maxima(2, 3)
                rotaries(0)
                maxima(4, 5, 6, 7)
                rotaries(1, 2)
                if project:
                    v_low(i, 0)
                rotaries(3)
                p_lows(0)
                if project:
                    v_low(i, 1)
                p_lows(2)
                out(0)
                if project:
                    last_rotary_sum(i)
                p_lows(4)
                out(1)
                if attend and is_first(g):
                    low(w_2[:, 1], stage_w2, w_2[:, 0], W_SCALE, 7)
                if mlp2:
                    gate_2(i - 2, 0)
                p_lows(6, 7)
                if project:
                    v_low(i, 2)
                out(2, 3)
                if project:
                    v_low(i, 3)
                stats1(0, 1, 2, 3)
                if mlp2:
                    gate_2(i - 2, 1)
                if norm_next:
                    norm_var(0, i + 1, ln1_stats, ln1_var)
                if is_first(i):
                    late_modulation()
                if attend:
                    for t in range(T):
                        gate_1(g, t)
                    norm_stat(1, g, x_mid, 0, mid_done, g * T + 1, ln2_stats)
                    norm_stat(1, g, x_mid, 1, mid_done, g * T + 2, ln2_stats)
                    norm_stat(1, g, x_mid, 2, mid_done, g * T + 3, ln2_stats)
                    norm_stat(1, g, x_mid, 3, mid_done, g * T + 4, ln2_stats)
                    norm_var(1, g, ln2_stats, ln2_var)
                    if not is_first(g):
                        dve.wait_ge(ln2_lo, g * T)
                    norm_factor(1, g, x_mid, mod2, 1, n2_32, ln2_factor, 0, 3)
                    norm_shift(1, g, mod2, 1, n2_32, ln2_factor, ln2_rstd, ln2_done, 0, 1)
                    norm_factor(1, g, x_mid, mod2, 1, n2_32, ln2_factor, 3, T)
                    norm_shift(1, g, mod2, 1, n2_32, ln2_factor, ln2_rstd, ln2_done, 1, T)
                if mlp2:
                    gate_2(i - 2, 2)
                if project:
                    k_low(i, 2)
                    k_low(i, 3)
                if norm_next:
                    norm1_factor(i + 1)
                    norm1_shift(i + 1)
                if mlp2:
                    gate_2(i - 2, 3)

                def low_hidden(u):
                    if attend:
                        h_low(g, u)

                def copy_n1(t):
                    if norm_next:
                        n1_copy_out(i + 1, t)

                low_hidden(0)
                copy_n1(0)
                if project:
                    double_high(i, q_stack, 32, True)
                copy_n1(1)
                low_hidden(2)
                copy_n1(2)
                if project:
                    double_high(i, k_stack, 64, False)
                copy_n1(3)
                low_hidden(4)

            iteration(0, True, False, False, True)
            low(w_1[:, 1], stage_w1, w_1[:, 0], W_SCALE, 6)
            iteration(1, True, True, False, True)
            iteration(2, True, True, True, True)
            with dve.Fori(3, G - 1) as i:
                iteration(i, True, True, True, True)
            iteration(G - 1, True, True, True, False)
            iteration(G, False, True, True, False)
            iteration(G + 1, False, False, True, False)

        @block.tensor
        def _(pe):
            PARTS = ((0, 0), (0, 1), (1, 0))

            pe.wait_ge(ident_done, 2)
            pe.wait_ge(cond_step, 3)
            for kt in range(KT):
                mm = pe.transpose(ps_score[0][:, kt * P:kt * P + P], cond_s[:, kt * P:kt * P + P], ident32[:])
            mm.then_inc(condT_ps, 1)
            pe.wait_ge(condT_done, 1)
            def modulation(ps, w):
                for kt in range(KT):
                    mm = pe.matmul(ps[:], condT[:, kt], w[:, kt], start=(kt == 0), stop=(kt == KT - 1))
                mm.then_inc(mod_ps, 1)

            pe.wait_ge(ada1_in, 16 * 4)
            modulation(ps_proj[0], stage_ada_a[:, :, 0:2 * C])
            pe.wait_ge(mod1_step, 1)
            pe.wait_ge(w_lo, 6)

            def turn(t, src, done):
                for part in range(2):
                    for kt in range(KT):
                        mm = pe.transpose(ps_turn[t % 2][:, part, kt], src[:, part, kt * P:kt * P + P], ident16[:])
                mm.then_inc(done, 1)

            def qk_unit(i, c):
                if c >= 2:
                    pe.wait_ge(rope_half, i * 8 + 2 * c - 2)
                elif c == 0 and not is_first(i) and not is_first(i - 1):
                    pe.wait_ge(gelu_done, (i - 1) * FU)
                w = w_qk[:, :, c // 2, :, (c % 2) * P:(c % 2) * P + P]
                for n, (a, b) in enumerate(PARTS):
                    for kt in range(KT):
                        mm = pe.matmul(ps_proj[c % 2][:], w[:, a, kt], n1T[:, b, kt],
                                       start=(n == 0 and kt == 0), stop=(n == 2 and kt == KT - 1))
                mm.then_inc(qk_ps, 1)

            def v_unit(i, q, mlp2):
                if q == 2:
                    pe.wait_ge(v_lo, i * BP + 2)
                elif q == 3:
                    if mlp2:
                        pe.wait_ge(gated2, (i - 2) * T + 1)
                    else:
                        pe.wait_ge(v_lo, i * BP + 1)
                elif q == 0 and not is_first(i) and not is_first(i - 1):
                    pe.wait_ge(gated1, (i - 1) * T)
                    if mlp2 and not is_first(i - 2):
                        pe.wait_ge(gated2, (i - 2) * T)
                for n, (a, b) in enumerate(PARTS):
                    for kt in range(KT):
                        mm = pe.matmul(tok_v(q), n1T[:, a, kt, q * P:q * P + P], w_v[:, b, kt],
                                       start=(n == 0 and kt == 0), stop=(n == 2 and kt == KT - 1))
                mm.then_inc(v_ps, 1)

            def mlp1_columns(g, u, cols):
                for n, (a, b) in enumerate(PARTS):
                    for kt in range(KT):
                        mm = pe.matmul(ps_proj[u % 2][:, cols], w_1[:, a, kt, u * P:u * P + P], n2T[:, b, kt, cols],
                                       start=(n == 0 and kt == 0), stop=(n == 2 and kt == KT - 1))
                return mm

            def mlp1_first_units(g, project):
                if is_first(g):
                    pe.wait_ge(w_lo, 9)
                if project:
                    pe.wait_ge(rope_half, (g + 2) * 8)
                for t in (1, 3):
                    pe.wait_ge(n2_out, g * T + t + 1)
                    for u in range(2):
                        mm = mlp1_columns(g, u, slice((t - 1) * P, (t + 1) * P))
                        if t == 3:
                            mm.then_inc(h_ps, 1)

            def mlp1_unit(g, u):
                pe.wait_ge(gelu_done, g * FU + u - 1)
                mlp1_columns(g, u, slice(0, GT)).then_inc(h_ps, 1)

            def mlp2_tile(g, t, project, attend, between=()):
                if t == 0:
                    if project:
                        pe.wait_ge(v_lo, (g + 2) * BP + 1)
                    else:
                        pe.wait_ge(gated1, (g + 1) * T)
                        pe.wait_ge(gated2, g * T)
                    for n in range(2):
                        pe.wait_ge(h_lo[n], (g + 1) * (FU // 2) - (0 if attend else 1))
                elif t == 1:
                    if project:
                        pe.wait_ge(v_lo, (g + 2) * BP + 3)
                elif attend:
                    pe.wait_ge(gated1, (g + 1) * T + t + 1)
                else:
                    pe.wait_ge(gated2, g * T + t - 1)
                for u in range(FU):
                    if t == 0 and u == FU - 2 and not attend:
                        for n in range(2):
                            pe.wait_ge(h_lo[n], (g + 1) * (FU // 2))
                    for n, (a, b) in enumerate(PARTS):
                        mm = pe.matmul(tok_mlp(t), h_16[:, u, a, t * P:t * P + P], w_2[:, b, u],
                                       start=(u == 0 and n == 0), stop=(u == FU - 1 and n == 2))
                    if u == FU - 1:
                        mm.then_inc(mlp_ps, 1)
                    elif u in between:
                        between[u]()

            def score_unit(g, s, project):
                q, half = s // 2, s % 2
                if s >= 2:
                    pe.wait_ge(smax_done, g * 8 + s - 1)
                elif s == 0:
                    pe.wait_ge(lo_stacked, (g + 1) * STACK_COUNT)
                    pe.wait_ge(hi_doubled, (g + 1) * 2)
                for j in range(JK):
                    for b in range(2):
                        jj, cols = JK * half + j, slice(N * (2 * q + b), N * (2 * q + b) + N)
                        mm = pe.matmul(ps_score[s % 2][N * b:N * b + N, 2 * N * j:2 * N * j + 2 * N],
                                       q_stack[0:96, jj, cols], k_stack[0:96, jj, 2 * q + b].rearrange("p a n -> p (a n)"),
                                       start=True, stop=True)
                mm.then_inc(s_ps, 1)

            def max_turn(g, q):
                pe.wait_ge(smax_done, g * 8 + 2 * q + 2)
                if q >= 2:
                    pe.wait_ge(smaxT_done, g * BP + q - 1)
                elif q == 0 and not is_first(g):
                    pe.wait_ge(o_done, g * BP)
                pe.transpose(ps_smaxT[q % 2], smax[:, q], ident32[:]).then_inc(smaxT_ps, 1)

            def softmax_unit(g, b):
                if b >= 2:
                    pe.wait_ge(exp_done, g * GB + b - 1)
                elif b == 0:
                    pe.wait_ge(smax_done, g * 8 + 8)
                if b % 4 == 0:
                    pe.wait_ge(smax_stacked[b // 4], g * 32 + 32)
                cols = slice(N * b, N * b + N)
                for j in range(J):
                    mm = pe.matmul(ps_score[b % 2][:, N * j:N * j + N], k_stack[0:98, j, b].rearrange("p a n -> p (a n)"),
                                   q_stack[0:98, j, cols], start=True, stop=True)
                mm.then_inc(st_ps, 1)

            def pv_unit(g, q):
                pe.wait_ge(*p_low_made(g, 2 * q))
                pe.wait_ge(*p_low_made(g, 2 * q + 1))
                if q >= 2:
                    pe.wait_ge(o_done, g * BP + q - 1)
                elif q == 0:
                    pe.wait_ge(v_stacked, g * 64 + 64)
                    pe.wait_ge(smaxT_done, g * BP + BP)
                for b in range(2):
                    for j in range(J):
                        for n, (a, c) in enumerate(PARTS):
                            mm = pe.matmul(pv_out[q % 2][N * b:N * b + N, 2 * j:2 * j + 2, :],
                                           p_16[:, (2 * q + b) % 4, a, N * j:N * j + N],
                                           v_diag[:, 2 * q + b, :, c, j, :], start=(n == 0), stop=(n == 2))
                mm.then_inc(pv_ps, 1)

            def wo_unit(g, t, project, mlp2):
                if t == 0:
                    if is_first(g):
                        pe.wait_ge(w_lo, 7)
                    pe.wait_ge(o_out, g * BP + BP)
                    if project:
                        pe.wait_ge(v_lo, (g + 2) * BP)
                    else:
                        pe.wait_ge(gated2, (g - 1) * T + 1)
                elif t == 1 and mlp2:
                    pe.wait_ge(gated2, (g - 1) * T + 2)
                elif t >= 2:
                    pe.wait_ge(gated1, g * T + t - 1)
                for n, (a, b) in enumerate(PARTS):
                    for kt in range(KT):
                        mm = pe.matmul(tok_wo(t), oT[:, a, kt, t * P:t * P + P], w_o[:, b, kt],
                                       start=(n == 0 and kt == 0), stop=(n == 2 and kt == KT - 1))
                mm.then_inc(attn_ps, 1)

            def iteration(i, project, attend, mlp2, norm_next):
                g = i - 1

                def qk(u):
                    if project:
                        qk_unit(i, u)

                def vv(*qs):
                    if project:
                        for q in qs:
                            v_unit(i, q, mlp2)

                def scores(*ss):
                    if attend:
                        for s in ss:
                            score_unit(g, s, project)

                def maxima(*qs):
                    if attend:
                        for q in qs:
                            max_turn(g, q)

                def soft(*bs):
                    if attend:
                        for b in bs:
                            softmax_unit(g, b)

                def pv(q):
                    if attend:
                        pv_unit(g, q)

                def mlp2_tiles(*ts):
                    if mlp2:
                        for t in ts:
                            mlp2_tile(i - 2, t, project, attend)

                def turn_o(*qs):
                    if attend:
                        for q in qs:
                            if q >= 2:
                                pe.wait_ge(o_out, g * BP + q - 1)
                            else:
                                pe.wait_ge(exp_done, g * GB + 7 + q)
                            pe.wait_ge(o_lo, g * BP + q + 1)
                            turn(q, o_16[:, q], o_turned)

                def turn_n1(*ts):
                    if norm_next:
                        for t in ts:
                            if t >= 2:
                                pe.wait_ge(n1_out, (i + 1) * T + t - 1)
                            pe.wait_ge(ln1_lo, (i + 1) * T + t + 1)
                            turn(t, n1_16[:, t], n1_turned)

                def turn_n2(*ts):
                    if attend:
                        for t in ts:
                            if t >= 2:
                                pe.wait_ge(n2_out, g * T + t - 1)
                            pe.wait_ge(ln2_lo, g * T + t + 1)
                            turn(t, n2_16[:, t], n2_turned)

                if project:
                    pe.wait_ge(n1_out, i * T + T)
                scores(0, 1)
                qk(0)
                scores(2, 3)
                qk(1)
                scores(4, 5)
                maxima(0, 1)
                vv(0)
                scores(6, 7)
                qk(2)
                maxima(2, 3)
                soft(0, 1)
                qk(3)
                soft(2, 3)
                vv(1)

                def next_scores(q):
                    pv(q)
                    soft(2 * q + 4, 2 * q + 5)

                if mlp2:
                    mlp2_tile(i - 2, 0, project, attend, {2: lambda: next_scores(0), 5: lambda: next_scores(1)})
                else:
                    next_scores(0)
                    next_scores(1)
                vv(2)
                pv(2)
                turn_o(0)
                vv(3)
                pv(3)
                turn_o(1)
                if mlp2:
                    mlp2_tile(i - 2, 1, project, attend, {2: lambda: turn_o(2), 5: lambda: turn_o(3)})
                else:
                    turn_o(2, 3)
                if attend:
                    for t in range(T):
                        wo_unit(g, t, project, mlp2)
                mlp2_tiles(2)
                if mlp2:
                    mlp2_tile(i - 2, 3, project, attend,
                              {5: lambda: turn_n2(0), 6: lambda: turn_n2(1)})
                else:
                    turn_n2(0, 1)
                turn_n2(2, 3)
                if attend:
                    mlp1_first_units(g, project)
                    for u in range(2, FU):
                        mlp1_unit(g, u)
                        if 2 <= u < T + 2:
                            turn_n1(u - 2)
                else:
                    if is_first(i):
                        pe.wait_ge(ada2_in, 16 * 4)
                        modulation(ps_pv[0], stage_ada_a[:, :, 2 * C:4 * C])
                        modulation(ps_pv[1], stage_ada_b)
                    turn_n1(0, 1, 2, 3)

            for t in range(T):
                if t >= 2:
                    pe.wait_ge(n1_out, t - 1)
                pe.wait_ge(ln1_lo, t + 1)
                turn(t, n1_16[:, t], n1_turned)
            iteration(0, True, False, False, True)
            pe.wait_ge(mod2_step, 2)
            iteration(1, True, True, False, True)
            iteration(2, True, True, True, True)
            with pe.Fori(3, G - 1) as i:
                iteration(i, True, True, True, True)
            iteration(G - 1, True, True, True, False)
            iteration(G, False, True, True, False)
            iteration(G + 1, False, False, True, False)


_INS = ['x', 'cond_1024', 'L0_cond_norm1_g', 'L0_cond_norm1_b', 'L0_cond_Wq', 'L0_cond_Wk', 'L0_cond_Wv',
        'L0_cond_Wo', 'L0_cond_norm2_g', 'L0_cond_norm2_b', 'L0_cond_W1', 'L0_cond_W2', 'L0_cond_ada_W',
        'L0_cond_ada_b']


def rope_table():
    dim = np.arange(P) % D
    inv_freq = (1.0 / 10000.0 ** (np.arange(0, D, 2, dtype=np.float32) / D)).astype(np.float32)
    t, i = np.meshgrid(np.arange(T), np.arange(I), indexing="ij")
    pos = (T * i + t).reshape(-1).astype(np.float32)
    angle = (pos[None, :] * inv_freq[dim % (D // 2)][:, None]).astype(np.float32)
    sign = np.where(dim < D // 2, -1.0, 1.0).astype(np.float32)[:, None]
    table = np.stack([np.cos(angle), sign * np.sin(angle)], axis=1) * ROPE_SCALE
    head = np.arange(P) // D
    parity = np.stack([head % 2 == 0, head % 2 == 1], axis=1)
    return np.ascontiguousarray(np.concatenate([table.reshape(P, 2 * N), parity], axis=1).astype(np.float32))


def kernel(**inputs):
    import concourse.bacc as _bacc
    from concourse import mybir as _mybir
    from concourse.bass_utils import run_bass_kernel_spmd as _run

    nc = _bacc.Bacc("TRN2", target_bir_lowering=False, num_devices=1)
    arrays, args = {}, []
    for name in _INS + ["rope"]:
        a = rope_table() if name == "rope" else np.ascontiguousarray(inputs[name])
        arrays[f"in_{name}_dram"] = a
        args.append(nc.dram_tensor(f"in_{name}_dram", a.shape, _mybir.dt.from_np(a.dtype), kind="ExternalInput").ap())
    args.append(nc.dram_tensor("out_0_dram", (B, N, C), F32, kind="ExternalOutput").ap())
    build(nc, *args)
    r = _run(nc, [arrays], core_ids=[0])
    return r.results[0]["out_0_dram"]
```
